# Optimizing a Trainium2 kernel written in Bass

```python
import numpy as np
import jax
import jax.numpy as jnp

def _softmax(x, axis=-1):
    return jax.nn.softmax(x, axis=axis)

def _gelu(x):
    return jax.nn.gelu(x, approximate=True)

def _silu(x):
    return jax.nn.silu(x)

def _sigmoid(x):
    return jax.nn.sigmoid(x)

def _layernorm(x, axis=-1, eps=1e-05):
    m = jnp.mean(x, axis=axis, keepdims=True)
    v = jnp.var(x, axis=axis, keepdims=True)
    return (x - m) / jnp.sqrt(v + eps)

def _scatter_add(tgt, idx, src, axis=0):
    return tgt.at[idx].add(src)

def _segment_sum(src, seg, n):
    return jax.ops.segment_sum(src, seg, n)
kernel_name = 'mk_adj_resnorm_d1_adj_r2_3b1262'

def setup_inputs(seed: int=0):
    np.random.seed(seed)
    _w = jnp.asarray

    def _rec_inputs():
        import jax
        import jax.numpy as jnp
        _gk = jax.random.key(seed)
        x = -0.0002928 + 1 * jax.random.normal(jax.random.fold_in(_gk, 1), (16, 512, 256), jnp.float32)
        _w = (1.0 + jnp.arange(512, dtype=jnp.float32)) ** (-0.5)
        _w = _w / _w.mean()
        _pij = jnp.clip(0.015625 * _w[:, None] * _w[None, :], 0.0, 1.0)
        _a = jax.random.uniform(jax.random.fold_in(_gk, 2), (16, 512, 512)) < _pij
        _a = jnp.logical_or(_a, jnp.swapaxes(_a, -1, -2))
        _a = jnp.logical_or(_a, jnp.eye(512, dtype=bool))
        _af = _a.astype(jnp.float32)
        _af = _af * jax.random.uniform(jax.random.fold_in(_gk, 3), (16, 512, 512), jnp.float32, 0.05, 1)
        adj = _af
        return (x, adj)
    x, adj = _rec_inputs()

    def _L0_gnn_setup():
        import jax, jax.numpy as jnp
        import numpy as np
        B, N, DIN, DOUT, K = (4, 1024, 256, 256, 3)
        key = jax.random.key(seed)
        ks = jax.random.split(key, 8)
        X = jax.random.normal(ks[0], (B, N, DIN), dtype=jnp.float32)
        A = jax.random.uniform(ks[1], (B, N, N), dtype=jnp.float32)
        Wv = jax.random.normal(ks[2], (DIN, DOUT), dtype=jnp.float32) * 0.02
        bv = jax.random.normal(ks[3], (DOUT,), dtype=jnp.float32) * 0.02
        aw = jax.random.normal(ks[4], (2 * DOUT, 1), dtype=jnp.float32) * 0.05
        ab = jax.random.normal(ks[5], (1,), dtype=jnp.float32) * 0.05
        Wk = jax.random.normal(ks[6], (K, DIN, DOUT), dtype=jnp.float32) * 0.02
        bk = jax.random.normal(ks[7], (K, DOUT), dtype=jnp.float32) * 0.02
        return {'X': X, 'A': A, 'Wv': Wv, 'bv': bv, 'aw': aw, 'ab': ab, 'Wk': Wk, 'bk': bk}
    _L0_gnn_all = _L0_gnn_setup()
    _L0_gnn_in = {k: v for k, v in _L0_gnn_all.items() if k in ('Wv', 'bv', 'aw', 'ab', 'Wk', 'bk')}
    del _L0_gnn_all
    return {'x': x, 'adj': adj, 'L0_gnn_Wv': _L0_gnn_in['Wv'], 'L0_gnn_bv': _L0_gnn_in['bv'], 'L0_gnn_aw': _L0_gnn_in['aw'], 'L0_gnn_ab': _L0_gnn_in['ab'], 'L0_gnn_Wk': _L0_gnn_in['Wk'], 'L0_gnn_bk': _L0_gnn_in['bk']}

def reference(x, adj, L0_gnn_Wv, L0_gnn_bv, L0_gnn_aw, L0_gnn_ab, L0_gnn_Wk, L0_gnn_bk):
    import jax
    import jax.numpy as jnp

    def _L0_gnn_ref(X, A, Wv, bv, aw, ab, Wk, bk):
        import jax, jax.numpy as jnp
        import numpy as np
        B, N, DIN, DOUT, K = (4, 1024, 256, 256, 3)
        d = Wv.shape[1]
        Xw = X @ Wv + bv
        sj = Xw @ aw[:d, 0]
        si = Xw @ aw[d:, 0]
        e = jax.nn.leaky_relu(sj[:, None, :] + si[:, :, None] + ab[0], negative_slope=0.2)
        alpha_matrix = A * jnp.exp(e)
        transition = alpha_matrix / (jnp.sum(alpha_matrix, axis=-1, keepdims=True) + 1e-12)
        H = jnp.zeros(X.shape[:-1] + (d,), dtype=X.dtype)
        Xk = X
        for k in range(Wk.shape[0]):
            H = H + Xk @ Wk[k] + bk[k]
            Xk = jnp.einsum('bij,bjd->bid', transition, Xk)
        return jax.nn.relu(H)
    x = _layernorm(x + _L0_gnn_ref(x, adj, L0_gnn_Wv, L0_gnn_bv, L0_gnn_aw, L0_gnn_ab, L0_gnn_Wk, L0_gnn_bk), axis=-1)
    return x

_drawn_inputs = setup_inputs


def setup_inputs(seed=0):
    import zlib

    import numpy as np

    out = dict(_drawn_inputs(seed))
    spreads = {}
    factors = {'L0_gnn_Wv': 4.355, 'L0_gnn_bv': 23.591, 'L0_gnn_aw': 4.428}
    for name, (base, spread) in spreads.items():
        noise = np.random.default_rng([zlib.crc32(name.encode()), seed]).standard_normal(out[name].shape)
        drawn = base * np.exp(spread * noise) if base else spread * noise
        out[name] = jnp.asarray(drawn.astype(out[name].dtype))
    for name, factor in factors.items():
        out[name] = (out[name] * factor).astype(out[name].dtype)
    return out
```

```python
from contextlib import ExitStack

import concourse.bass as bass
from concourse import mybir

ALU = mybir.AluOpType
ACT = mybir.ActivationFunctionType
F32 = mybir.dt.float32
F32R = mybir.dt.float32r

P = 128
ROWSUM_EPS = 1e-12
LN_EPS = 1e-5
PAR = 2


def build(nc, xT, adjT, x, Wv, bv, aw, ab, Wk, bk, out):
    G, N, D = x.shape
    NB = N // P
    KB = D // P
    STEPS = Wk.shape[0]
    assert NB == 4 and KB == 2 and STEPS == 3 and G % 2 == 0
    WA = 2 * D
    WB = D + 2
    SJ, SI = D, D + 1
    U1 = D + 2
    PAIR = NB // 2

    xT_of = xT.rearrange("(q u) p k n -> q u p k n", u=PAR)
    adjT_of = adjT.rearrange("(q u) p b n -> q u p b n", u=PAR)
    x_of = x.rearrange("(q u) (p b) d -> q u p (b d)", u=PAR, b=NB)
    out_of = out.rearrange("(q u) (p b) d -> q u p (b d)", u=PAR, b=NB)

    def done(g4, n):
        return g4 + n

    with ExitStack() as ctx:
        def sb(name, shape, dt=F32):
            return ctx.enter_context(nc.sbuf_tensor(name, shape, dt))

        def ps(name, shape):
            return ctx.enter_context(nc.psum_tensor(name, shape, F32))

        def sem(name):
            return ctx.enter_context(nc.semaphore(name))

        w_raw = sb("w_raw", [P, KB, WA + WB])
        w_hi = sb("w_hi", [P, KB, WA + WB], F32R)
        w_lo = sb("w_lo", [P, KB, WA + WB], F32R)
        wv = sb("wv", [P, KB, D])
        aw_row = sb("aw_row", [P, 2, D])
        bv_row = sb("bv_row", [P, D])
        bk_row = sb("bk_row", [P, STEPS, D])
        ab_col = sb("ab_col", [P, 1])
        aw_sum = sb("aw_sum", [P, D])
        b01_row = sb("b01_row", [P, D])
        product = sb("product", [P, 5, D])
        c_col = sb("c_col", [P, 1])
        bias_row = sb("bias_row", [P, WB])
        ident = sb("ident", [P, P])
        xT_in = [sb(f"xT_in{u}", [P, KB, N]) for u in range(PAR)]
        adj_in = [sb(f"adj_in{u}", [P, NB, N]) for u in range(PAR)]
        x_in = [sb(f"x_in{u}", [P, NB, D]) for u in range(PAR)]
        xT_hi = [sb(f"xT_hi{u}", [P, KB, N], F32R) for u in range(PAR)]
        xT_lo = [sb(f"xT_lo{u}", [P, KB, N], F32R) for u in range(PAR)]
        g0s = [sb(f"g0s{u}", [P, NB, WB]) for u in range(PAR)]
        g1 = [sb(f"g1_{u}", [P, NB, D]) for u in range(PAR)]
        factors = [sb(f"factors{u}", [P, NB, 2]) for u in range(PAR)]
        g2_hi = [sb(f"g2_hi{u}", [P, NB, U1], F32R) for u in range(PAR)]
        g2_lo = [sb(f"g2_lo{u}", [P, NB, U1], F32R) for u in range(PAR)]
        alpha = sb("alpha", [P, NB, N])
        al_hi = [sb(f"al_hi{u}", [P, NB, N], F32R) for u in range(PAR)]
        al_lo = [sb(f"al_lo{u}", [P, NB, N], F32R) for u in range(PAR)]
        denom = sb("denom", [P, NB])
        rcp = [sb(f"rcp{u}", [P, NB]) for u in range(PAR)]
        rcp_f = sb("rcp_f", [P, NB])
        v = sb("v", [P, NB, D])
        v_hi = sb("v_hi", [P, NB, D], F32R)
        v_lo = sb("v_lo", [P, NB, D], F32R)
        h = sb("h", [P, NB, D])
        y = sb("y", [P, NB, D])
        stats = sb("stats", [P, NB, 6])
        mean_gap = sb("mean_gap", [P, NB])
        mean_sum = sb("mean_sum", [P, NB])
        dev_sum = sb("dev_sum", [P, NB])
        gap_dev = sb("gap_dev", [P, NB])
        var = sb("var", [P, NB])
        minus_half = sb("minus_half", [P, PAIR])
        var_eps = sb("var_eps", [P, NB])
        minus_mean = sb("minus_mean", [P, NB])
        rstd = sb("rstd", [P, NB])
        shift = sb("shift", [P, NB])
        res = [sb(f"res{u}", [P, NB, D]) for u in range(PAR)]
        ps_a = ps("ps_a", [P, 2, WA])
        ps_b = ps("ps_b", [P, 512])
        ps_z = ps("ps_z", [P, N])
        ps_u = ps("ps_u", [P, NB, 512])

        w_loaded = sem("w_loaded")
        small_loaded = sem("small_loaded")
        xT_loaded = [sem(f"xT_loaded{u}") for u in range(PAR)]
        adj_loaded = [sem(f"adj_loaded{u}") for u in range(PAR)]
        x_loaded = [sem(f"x_loaded{u}") for u in range(PAR)]
        stored = [sem(f"stored{u}") for u in range(PAR)]
        zeroed = sem("zeroed")
        ident_ready = sem("ident_ready")
        setup = sem("setup")
        w_hi_ready = sem("w_hi_ready")
        w_ready = sem("w_ready")
        xh_ready = sem("xh_ready")
        x_split = sem("x_split")
        wa_done = sem("wa_done")
        wb_done = sem("wb_done")
        g1_ready = sem("g1_ready")
        g2_ready = sem("g2_ready")
        g0s_ready = sem("g0s_ready")
        z_done = sem("z_done")
        factors_done = sem("factors_done")
        fh_ready = sem("fh_ready")
        f_ready = sem("f_ready")
        rcpf_done = sem("rcpf_done")
        exp_done = sem("exp_done")
        alpha_done = sem("alpha_done")
        alh_ready = sem("alh_ready")
        al_ready = sem("al_ready")
        t1_done = sem("t1_done")
        denom_done = sem("denom_done")
        rcp_done = sem("rcp_done")
        v_done = sem("v_done")
        vh_ready = sem("vh_ready")
        v_ready = sem("v_ready")
        t2_done = sem("t2_done")
        h_done = sem("h_done")
        y_done = sem("y_done")
        stats_done = sem("stats_done")
        parts_done = sem("parts_done")
        gap_done = sem("gap_done")
        minus_done = sem("minus_done")
        eps_done = sem("eps_done")
        var_done = sem("var_done")
        mean_done = sem("mean_done")
        rstd_done = sem("rstd_done")
        norm_ready = sem("norm_ready")
        res_ready = sem("res_ready")

        SMALL = 16 * 5
        block = ctx.enter_context(nc.Block())

        LOOPED = 4 * (G - 2)

        @block.sync
        def _(sp):
            def load_xT(q, u, first=False):
                if not first:
                    sp.wait_ge(x_split, done(8 * q + 4 * u, -4))
                sp.dma_start(xT_in[u][:, :, :], xT_of[q, u]).then_inc(xT_loaded[u], 16)

            def load_adj(q, u, first=False):
                if not first:
                    sp.wait_ge(alpha_done, done(8 * q + 4 * u, -4))
                sp.dma_start(adj_in[u][:, :, :], adjT_of[q, u]).then_inc(adj_loaded[u], 16)

            def load_x(q, u, first=False):
                if not first:
                    sp.wait_ge(y_done, done(8 * q + 4 * u, -4))
                sp.dma_start(x_in[u][:, :, :].rearrange("p b d -> p (b d)"), x_of[q, u]).then_inc(x_loaded[u], 16)

            sp.dma_start(wv[:, :, :], Wv.rearrange("(k p) n -> p k n", p=P)).then_inc(small_loaded, 16)
            sp.dma_start(aw_row[:, :, :].rearrange("p a d -> p (a d)"),
                         aw.rearrange("n a -> a n").partition_broadcast(P)).then_inc(small_loaded, 16)
            load_xT(0, 0, first=True)
            sp.dma_start(w_raw[:, :, WA:WA + D], Wk[0].rearrange("(k p) n -> p k n", p=P)).then_inc(w_loaded, 16)
            sp.dma_start(bv_row[:, :], bv.partition_broadcast(P)).then_inc(small_loaded, 16)
            sp.dma_start(ab_col[:, :], ab.partition_broadcast(P)).then_inc(small_loaded, 16)
            sp.dma_start(bk_row[:, :, :], bk.partition_broadcast(P)).then_inc(small_loaded, 16)
            for k in range(1, STEPS):
                sp.dma_start(w_raw[:, :, (k - 1) * D:k * D], Wk[k].rearrange("(k p) n -> p k n", p=P))\
                    .then_inc(w_loaded, 16)
            load_adj(0, 0, first=True)
            load_xT(0, 1, first=True)
            load_adj(0, 1, first=True)
            for u in range(PAR):
                load_xT(1, u)
                load_adj(1, u)
                load_x(0, u, first=True)
            with sp.Fori(2, G // PAR, 1) as q:
                for u in range(PAR):
                    load_xT(q, u)
                    load_adj(q, u)
                    load_x(q - 1, u)
            for u in range(PAR):
                load_x(G // PAR - 1, u)

        @block.gpsimd
        def _(pool):
            nc.gpsimd.memset(ident[:, :], 0.0).then_inc(zeroed, 1)
            pool.wait_ge(zeroed, 1)
            nc.gpsimd.affine_select(out=ident[:, :], in_=ident[:, :], compare_op=ALU.not_equal, fill=1.0, base=0,
                                    pattern=[[-1, P]], channel_multiplier=1).then_inc(ident_ready, 1)
            nc.gpsimd.memset(minus_half[:, :], -0.5).then_inc(zeroed, 1)
            pool.wait_ge(zeroed, 2)

            def norm(g4, half):
                rows = slice(2 * half, 2 * half + 2)
                n = done(g4, 2 * half + 2)
                pool.wait_ge(mean_done, n)
                nc.gpsimd.tensor_scalar(minus_mean[:, rows], mean_sum[:, rows], -0.5, None, ALU.mult)\
                    .then_inc(minus_done, 2)
                pool.wait_ge(var_done, n)
                nc.gpsimd.tensor_scalar(var_eps[:, rows], var[:, rows], LN_EPS, None, ALU.add).then_inc(eps_done, 2)
                if half == 0 and (not isinstance(g4, int) or g4 > 0):
                    pool.wait_ge(res_ready, g4)
                pool.wait_ge(eps_done, n)
                nc.gpsimd.tensor_tensor(rstd[:, rows], var_eps[:, rows], minus_half[:, :], ALU.pow)\
                    .then_inc(rstd_done, 2)
                pool.wait_ge(minus_done, n)
                pool.wait_ge(rstd_done, n)
                nc.gpsimd.tensor_tensor(shift[:, rows], minus_mean[:, rows], rstd[:, rows], ALU.mult)\
                    .then_inc(norm_ready, 2)

            norm(0, 0)
            norm(0, 1)
            with pool.Fori(4, 4 * G, 4) as g4:
                norm(g4, 0)
                norm(g4, 1)

        @block.tensor
        def _(pe):
            def products_a(g4, u):
                pe.wait_ge(x_split, done(g4, 4))
                for b in range(NB):
                    if b >= 2 or not isinstance(g4, int) or g4 >= 4:
                        pe.wait_ge(g2_ready, done(g4, b - 1))
                    rows = slice(b * P, (b + 1) * P)
                    for k in range(KB):
                        bank = ps_a[:, b % 2, :]
                        nc.tensor.matmul(bank, xT_hi[u][:, k, rows], w_hi[:, k, 0:WA], start=k == 0, stop=False)
                        nc.tensor.matmul(bank, xT_hi[u][:, k, rows], w_lo[:, k, 0:WA], start=False, stop=False)
                        last = nc.tensor.matmul(bank, xT_lo[u][:, k, rows], w_hi[:, k, 0:WA], start=False,
                                                stop=k == KB - 1)
                    last.then_inc(wa_done, 1)

            def products_b(g4, u, b):
                if b == 0:
                    pe.wait_ge(x_split, done(g4, 4))
                if not isinstance(g4, int) or g4 + b > 0:
                    pe.wait_ge(g0s_ready, done(g4, b))
                rows = slice(b * P, (b + 1) * P)
                for k in range(KB):
                    bank = ps_b[:, 0:WB]
                    cols = slice(WA, WA + WB)
                    nc.tensor.matmul(bank, xT_hi[u][:, k, rows], w_hi[:, k, cols], start=k == 0, stop=False)
                    nc.tensor.matmul(bank, xT_hi[u][:, k, rows], w_lo[:, k, cols], start=False, stop=False)
                    last = nc.tensor.matmul(bank, xT_lo[u][:, k, rows], w_hi[:, k, cols], start=False,
                                            stop=k == KB - 1)
                last.then_inc(wb_done, 1)

            def spread_si(g4, u):
                pe.wait_ge(g0s_ready, done(g4, 4))
                if not isinstance(g4, int) or g4 > 0:
                    pe.wait_ge(exp_done, g4)
                for b in range(NB):
                    last = nc.tensor.transpose(ps_z[:, b * P:(b + 1) * P],
                                               g0s[u][:, b, SI:SI + 1].to_broadcast([P, P]), ident[:, :])
                last.then_inc(z_done, 4)

            def apply_1(g4, u, b):
                if b == 0:
                    pe.wait_ge(al_ready, done(g4, 4))
                    pe.wait_ge(g2_ready, done(g4, 4))
                    pe.wait_ge(f_ready, done(g4, 4))
                if not isinstance(g4, int) or g4 > 0:
                    pe.wait_ge(h_done, done(g4, b - 3))
                cols = slice(b * P, (b + 1) * P)
                for j in range(NB):
                    nc.tensor.matmul(ps_u[:, b, 0:U1], al_hi[u][:, j, cols], g2_hi[u][:, j, :], start=j == 0,
                                     stop=False)
                    nc.tensor.matmul(ps_u[:, b, 0:U1], al_hi[u][:, j, cols], g2_lo[u][:, j, :], start=False,
                                     stop=False)
                    last = nc.tensor.matmul(ps_u[:, b, 0:U1], al_lo[u][:, j, cols], g2_hi[u][:, j, :], start=False,
                                            stop=j == NB - 1)
                last.then_inc(t1_done, 1)

            def apply_2(g4, u, b):
                if b == 0:
                    pe.wait_ge(v_ready, done(g4, 4))
                cols = slice(b * P, (b + 1) * P)
                for j in range(NB):
                    nc.tensor.matmul(ps_u[:, b, 0:D], al_hi[u][:, j, cols], v_hi[:, j, :], start=j == 0, stop=False)
                    nc.tensor.matmul(ps_u[:, b, 0:D], al_hi[u][:, j, cols], v_lo[:, j, :], start=False, stop=False)
                    last = nc.tensor.matmul(ps_u[:, b, 0:D], al_lo[u][:, j, cols], v_hi[:, j, :], start=False,
                                            stop=j == NB - 1)
                last.then_inc(t2_done, 1)

            pe.wait_ge(w_ready, 1)
            for b in range(NB):
                products_b(0, 0, b)
            pe.wait_ge(ident_ready, 1)
            spread_si(0, 0)
            pe.wait_ge(w_ready, 2)
            products_a(0, 0)
            for b in range(NB):
                products_b(4, 1, b)
            spread_si(4, 1)
            for b in range(NB):
                apply_1(0, 0, b)
            with pe.Fori(0, LOOPED, 8) as pair4:
                for u in range(PAR):
                    g4 = pair4 + 4 * u
                    products_a(g4 + 4, 1 - u)
                    for b in range(NB):
                        apply_2(g4, u, b)
                        products_b(g4 + 8, u, b)
                    apply_1(g4 + 4, 1 - u, 0)
                    spread_si(g4 + 8, u)
                    for b in range(1, NB):
                        apply_1(g4 + 4, 1 - u, b)
            products_a(LOOPED + 4, 1)
            for b in range(NB):
                apply_2(LOOPED, 0, b)
            for b in range(NB):
                apply_1(LOOPED + 4, 1, b)
            for b in range(NB):
                apply_2(LOOPED + 4, 1, b)

        @block.scalar
        def _(act):
            def split_x(g4, u, loads):
                act.wait_ge(xT_loaded[u], loads)
                if not isinstance(g4, int) or g4 >= 8:
                    act.wait_ge(wa_done, done(g4, -4))
                nc.scalar.activation(xT_hi[u][:, :, :], xT_in[u][:, :, :], ACT.Copy).then_inc(xh_ready, 4)

            def leave_a(g4, u, b):
                act.wait_ge(wa_done, done(g4, b + 1))
                if b == 0 and (not isinstance(g4, int) or g4 >= 8):
                    act.wait_ge(t1_done, done(g4, -4))
                    act.wait_ge(v_done, done(g4, -4))
                f = factors[u][:, b, 0:1]
                nc.scalar.activation(g2_hi[u][:, b, 0:D], ps_a[:, b % 2, D:WA], ACT.Copy, scale=f)
                nc.scalar.activation(g1[u][:, b, :], ps_a[:, b % 2, 0:D], ACT.Copy, scale=f).then_inc(g1_ready, 1)

            def factor(g4, u):
                act.wait_ge(g0s_ready, done(g4, 4))
                if not isinstance(g4, int) or g4 >= 8:
                    act.wait_ge(v_done, done(g4, -4))
                nc.scalar.activation(factors[u][:, :, :], g0s[u][:, :, D:WB], ACT.Exp, scale=0.25)\
                    .then_inc(factors_done, 4)
                act.wait_ge(factors_done, done(g4, 4))
                nc.scalar.activation(g2_hi[u][:, :, D:U1], factors[u][:, :, :], ACT.Copy).then_inc(fh_ready, 4)

            def exponential(g4, u, b):
                if b == 0:
                    act.wait_ge(z_done, done(g4, 4))
                    if not isinstance(g4, int) or g4 > 0:
                        act.wait_ge(al_ready, g4)
                nc.scalar.activation(alpha[:, b, :], ps_z[:, :], ACT.Exp, scale=-1.0, bias=g0s[u][:, b, SJ:SJ + 1])\
                    .then_inc(exp_done, 1)

            def alpha_high(g4, u, half):
                act.wait_ge(alpha_done, done(g4, 2 * half + 2))
                if half == 0 and (not isinstance(g4, int) or g4 >= 8):
                    act.wait_ge(t2_done, done(g4, -4))
                rows = slice(2 * half, 2 * half + 2)
                nc.scalar.activation(al_hi[u][:, rows, :], alpha[:, rows, :], ACT.Copy).then_inc(alh_ready, 2)

            def v_high(g4, half):
                act.wait_ge(v_done, done(g4, 2 * half + 2))
                if half == 0 and (not isinstance(g4, int) or g4 > 0):
                    act.wait_ge(t2_done, g4)
                rows = slice(2 * half, 2 * half + 2)
                nc.scalar.activation(v_hi[:, rows, :], v[:, rows, :], ACT.Copy).then_inc(vh_ready, 2)

            def normalise(g4, u, half, stores):
                act.wait_ge(norm_ready, done(g4, 2 * half + 2))
                if half == 0 and (not isinstance(g4, int) or g4 >= 8):
                    act.wait_ge(stored[u], stores)
                for b in range(2 * half, 2 * half + 2):
                    nc.scalar.activation(res[u][:, b, :], y[:, b, :], ACT.Identity, bias=shift[:, b:b + 1],
                                         scale=rstd[:, b:b + 1]).then_inc(res_ready, 1)

            def store(q, g4, u):
                act.wait_ge(res_ready, done(g4, 4))
                act.dma_start(out_of[q, u], res[u][:, :, :].rearrange("p b d -> p (b d)")).then_inc(stored[u], 16)

            split_x(0, 0, 16)
            act.wait_ge(setup, 4)
            act.wait_ge(w_loaded, 16 * STEPS)
            nc.scalar.activation(w_hi[:, :, WA:], w_raw[:, :, WA:], ACT.Copy).then_inc(w_hi_ready, 1)
            nc.scalar.activation(w_hi[:, :, 0:WA], w_raw[:, :, 0:WA], ACT.Copy).then_inc(w_hi_ready, 1)
            factor(0, 0)
            for b in range(NB):
                exponential(0, 0, b)
            leave_a(0, 0, 0)
            leave_a(0, 0, 1)
            split_x(4, 1, 16)
            leave_a(0, 0, 2)
            alpha_high(0, 0, 0)
            leave_a(0, 0, 3)
            alpha_high(0, 0, 1)

            def step(q, g4, u, follow, xT_loads, stores):
                if follow >= 1:
                    factor(g4 + 4, 1 - u)
                v_high(g4, 0)
                v_high(g4, 1)
                if follow >= 1:
                    leave_a(g4 + 4, 1 - u, 0)
                    exponential(g4 + 4, 1 - u, 0)
                    leave_a(g4 + 4, 1 - u, 1)
                if follow >= 2:
                    split_x(g4 + 8, u, xT_loads)
                if follow >= 1:
                    leave_a(g4 + 4, 1 - u, 2)
                    exponential(g4 + 4, 1 - u, 1)
                    leave_a(g4 + 4, 1 - u, 3)
                    exponential(g4 + 4, 1 - u, 2)
                    exponential(g4 + 4, 1 - u, 3)
                    alpha_high(g4 + 4, 1 - u, 0)
                    alpha_high(g4 + 4, 1 - u, 1)
                normalise(g4, u, 0, stores)
                normalise(g4, u, 1, stores)
                store(q, g4, u)

            for u in range(PAR):
                step(0, 4 * u, u, 2, 32, 0)
            with act.Fori(1, G // PAR - 1, 1) as q:
                for u in range(PAR):
                    step(q, 8 * q + 4 * u, u, 2, 16 * q + 32, 16 * q)
            step(G // PAR - 1, LOOPED, 0, 1, 0, 8 * (G - 2))
            step(G // PAR - 1, LOOPED + 4, 1, 0, 0, 8 * (G - 2))
            for u in range(PAR):
                act.wait_ge(stored[u], 8 * G)

        @block.vector
        def _(dve):
            def split_x(g4, u):
                dve.wait_ge(xh_ready, done(g4, 4))
                nc.vector.tensor_tensor(xT_lo[u][:, :, :], xT_in[u][:, :, :], xT_hi[u][:, :, :].bitcast(F32),
                                        ALU.subtract).then_inc(x_split, 4)

            def leave_b(g4, u, b):
                dve.wait_ge(wb_done, done(g4, b + 1))
                if not isinstance(g4, int) or g4 >= 8:
                    dve.wait_ge(h_done, done(g4, b - 7))
                nc.vector.tensor_tensor(g0s[u][:, b, :], ps_b[:, 0:WB], bias_row[:, :], ALU.add)\
                    .then_inc(g0s_ready, 1)

            def g2_low(g4, u, b):
                dve.wait_ge(g1_ready, done(g4, b + 1))
                nc.vector.scalar_tensor_tensor(g2_lo[u][:, b, 0:D], ps_a[:, b % 2, D:WA], factors[u][:, b, 0:1],
                                               g2_hi[u][:, b, 0:D].bitcast(F32), ALU.mult, ALU.subtract)\
                    .then_inc(g2_ready, 1)

            def f_low(g4, u):
                dve.wait_ge(fh_ready, done(g4, 4))
                nc.vector.tensor_tensor(g2_lo[u][:, :, D:U1], factors[u][:, :, :],
                                        g2_hi[u][:, :, D:U1].bitcast(F32), ALU.subtract).then_inc(f_ready, 4)

            def times_adj(g4, u, half, loads):
                dve.wait_ge(exp_done, done(g4, 2 * half + 2))
                if half == 0:
                    dve.wait_ge(adj_loaded[u], loads)
                two = alpha[:, 2 * half:2 * half + 2, :]
                nc.vector.scalar_tensor_tensor(two, two, 1.0, adj_in[u][:, 2 * half:2 * half + 2, :], ALU.max,
                                               ALU.mult)\
                    .then_inc(alpha_done, 2)

            def alpha_low(g4, u, half):
                dve.wait_ge(alh_ready, done(g4, 2 * half + 2))
                rows = slice(2 * half, 2 * half + 2)
                nc.vector.tensor_tensor(al_lo[u][:, rows, :], alpha[:, rows, :], al_hi[u][:, rows, :].bitcast(F32),
                                        ALU.subtract).then_inc(al_ready, 2)

            def combine(g4, u, half):
                rows = slice(2 * half, 2 * half + 2)
                dve.wait_ge(t1_done, done(g4, 2 * half + 2))
                nc.vector.scalar_tensor_tensor(denom[:, rows], factors[u][:, rows, 1], ROWSUM_EPS, ps_u[:, rows, D],
                                               ALU.mult, ALU.add)\
                    .then_inc(denom_done, 2)
                dve.wait_ge(denom_done, done(g4, 2 * half + 2))
                nc.vector.reciprocal(rcp[u][:, rows], denom[:, rows]).then_inc(rcp_done, 2)
                dve.wait_ge(rcp_done, done(g4, 2 * half + 2))
                nc.vector.tensor_tensor(rcp_f[:, rows], rcp[u][:, rows], factors[u][:, rows, 0], ALU.mult)\
                    .then_inc(rcpf_done, 2)
                dve.wait_ge(rcpf_done, done(g4, 2 * half + 2))
                for b in range(2 * half, 2 * half + 2):
                    nc.vector.scalar_tensor_tensor(v[:, b, :], ps_u[:, b, 0:D], rcp_f[:, b:b + 1], g1[u][:, b, :],
                                                   ALU.mult, ALU.add).then_inc(v_done, 1)

            def v_low(g4, half):
                dve.wait_ge(vh_ready, done(g4, 2 * half + 2))
                rows = slice(2 * half, 2 * half + 2)
                nc.vector.tensor_tensor(v_lo[:, rows, :], v[:, rows, :], v_hi[:, rows, :].bitcast(F32),
                                        ALU.subtract).then_inc(v_ready, 2)

            def hidden(g4, u, b):
                dve.wait_ge(t2_done, done(g4, b + 1))
                nc.vector.scalar_tensor_tensor(h[:, b, :], ps_u[:, b, 0:D], rcp[u][:, b:b + 1], g0s[u][:, b, 0:D],
                                               ALU.mult, ALU.add).then_inc(h_done, 1)

            def residual(g4, u, half, loads):
                rows = slice(2 * half, 2 * half + 2)
                n = done(g4, 2 * half + 2)
                dve.wait_ge(h_done, n)
                if half == 0:
                    dve.wait_ge(x_loaded[u], loads)
                    if not isinstance(g4, int) or g4 > 0:
                        dve.wait_ge(res_ready, g4)
                nc.vector.scalar_tensor_tensor(y[:, rows, :], h[:, rows, :], 0.0, x_in[u][:, rows, :],
                                               ALU.max, ALU.add).then_inc(y_done, 2)
                dve.wait_ge(y_done, n)
                for b in range(2 * half, 2 * half + 2):
                    nc.vector.bn_stats(stats[:, b, :], y[:, b, :]).then_inc(stats_done, 1)
                dve.wait_ge(stats_done, n)
                if half == 0 and (not isinstance(g4, int) or g4 > 0):
                    dve.wait_ge(norm_ready, g4)
                even_mean, odd_mean = stats[:, rows, 1], stats[:, rows, 4]
                even_dev, odd_dev = stats[:, rows, 2], stats[:, rows, 5]
                nc.vector.tensor_tensor(mean_gap[:, rows], even_mean, odd_mean, ALU.subtract).then_inc(parts_done, 2)
                nc.vector.tensor_tensor(dev_sum[:, rows], even_dev, odd_dev, ALU.add).then_inc(parts_done, 2)
                nc.vector.tensor_tensor(mean_sum[:, rows], even_mean, odd_mean, ALU.add).then_inc(mean_done, 2)
                dve.wait_ge(parts_done, 2 * g4 + 4 * half + 4)
                nc.vector.scalar_tensor_tensor(gap_dev[:, rows], mean_gap[:, rows], 0.25, mean_gap[:, rows],
                                               ALU.mult, ALU.mult).then_inc(gap_done, 2)
                dve.wait_ge(gap_done, n)
                nc.vector.scalar_tensor_tensor(var[:, rows], dev_sum[:, rows], 1.0 / D, gap_dev[:, rows],
                                               ALU.mult, ALU.add).then_inc(var_done, 2)

            nc.vector.memset(bias_row[:, SI:SI + 1], 0.0)
            dve.wait_ge(small_loaded, SMALL)
            for k in range(KB):
                for a in range(2):
                    nc.vector.tensor_tensor_reduce(out=product[:, 2 * k + a, :], in0=wv[:, k, :], in1=aw_row[:, a, :],
                                                   scale=0.8 if a == 0 else -0.8, scalar=0.0, op0=ALU.mult, op1=ALU.add,
                                                   accum_out=w_raw[:, k, WA + D + a:WA + D + a + 1])\
                        .then_inc(setup, 1)
            dve.wait_ge(w_hi_ready, 1)
            nc.vector.tensor_tensor(w_lo[:, :, WA:], w_raw[:, :, WA:], w_hi[:, :, WA:].bitcast(F32), ALU.subtract)\
                .then_inc(w_ready, 1)
            split_x(0, 0)
            nc.vector.tensor_tensor(aw_sum[:, :], aw_row[:, 0, :], aw_row[:, 1, :], ALU.add).then_inc(setup, 1)
            nc.vector.tensor_tensor(b01_row[:, :], bk_row[:, 0, :], bk_row[:, 1, :], ALU.add).then_inc(setup, 1)
            dve.wait_ge(setup, 6)
            nc.vector.tensor_tensor_reduce(out=product[:, 4, :], in0=bv_row[:, :], in1=aw_sum[:, :], scale=0.8,
                                           scalar=0.0, op0=ALU.mult, op1=ALU.add, accum_out=c_col[:, :])\
                .then_inc(setup, 1)
            nc.vector.tensor_tensor(bias_row[:, 0:D], b01_row[:, :], bk_row[:, 2, :], ALU.add).then_inc(setup, 1)
            dve.wait_ge(setup, 8)
            nc.vector.scalar_tensor_tensor(bias_row[:, SJ:SJ + 1], ab_col[:, :], 0.8, c_col[:, :], ALU.mult, ALU.add)\
                .then_inc(setup, 1)
            dve.wait_ge(setup, 9)
            leave_b(0, 0, 0)
            leave_b(0, 0, 1)
            leave_b(0, 0, 2)
            leave_b(0, 0, 3)
            dve.wait_ge(w_hi_ready, 2)
            nc.vector.tensor_tensor(w_lo[:, :, 0:WA], w_raw[:, :, 0:WA], w_hi[:, :, 0:WA].bitcast(F32), ALU.subtract)\
                .then_inc(w_ready, 1)
            f_low(0, 0)
            g2_low(0, 0, 0)
            g2_low(0, 0, 1)
            times_adj(0, 0, 0, 16)
            split_x(4, 1)
            g2_low(0, 0, 2)
            times_adj(0, 0, 1, 16)
            g2_low(0, 0, 3)
            alpha_low(0, 0, 0)
            alpha_low(0, 0, 1)
            for b in range(NB):
                leave_b(4, 1, b)
            combine(0, 0, 0)
            combine(0, 0, 1)

            def step(g4, u, follow, x_loads, adj_loads):
                if follow >= 1:
                    f_low(g4 + 4, 1 - u)
                v_low(g4, 0)
                if follow >= 1:
                    g2_low(g4 + 4, 1 - u, 0)
                v_low(g4, 1)
                if follow >= 1:
                    g2_low(g4 + 4, 1 - u, 1)
                if follow >= 2:
                    split_x(g4 + 8, u)
                if follow >= 1:
                    g2_low(g4 + 4, 1 - u, 2)
                    g2_low(g4 + 4, 1 - u, 3)
                    times_adj(g4 + 4, 1 - u, 0, adj_loads)
                hidden(g4, u, 0)
                if follow >= 2:
                    leave_b(g4 + 8, u, 0)
                if follow >= 1:
                    times_adj(g4 + 4, 1 - u, 1, adj_loads)
                hidden(g4, u, 1)
                if follow >= 2:
                    leave_b(g4 + 8, u, 1)
                if follow >= 1:
                    alpha_low(g4 + 4, 1 - u, 0)
                    alpha_low(g4 + 4, 1 - u, 1)
                else:
                    residual(g4, u, 0, x_loads)
                hidden(g4, u, 2)
                if follow >= 2:
                    leave_b(g4 + 8, u, 2)
                hidden(g4, u, 3)
                if follow >= 2:
                    leave_b(g4 + 8, u, 3)
                if follow >= 1:
                    residual(g4, u, 0, x_loads)
                residual(g4, u, 1, x_loads)
                if follow >= 1:
                    combine(g4 + 4, 1 - u, 0)
                    combine(g4 + 4, 1 - u, 1)

            for u in range(PAR):
                step(4 * u, u, 2, 16, 16 * (1 + u))
            with dve.Fori(8, LOOPED, 8) as pair4:
                for u in range(PAR):
                    step(pair4 + 4 * u, u, 2, 2 * pair4 + 16, 2 * pair4 + 16 * (1 + u))
            step(LOOPED, 0, 1, 8 * G, 8 * G)
            step(LOOPED + 4, 1, 0, 8 * G, 8 * G)


def kernel(x, adj, L0_gnn_Wv, L0_gnn_bv, L0_gnn_aw, L0_gnn_ab, L0_gnn_Wk, L0_gnn_bk):
    import numpy as np
    import concourse.bacc as bacc
    from concourse.bass_utils import run_bass_kernel_spmd

    x, adj = np.asarray(x), np.asarray(adj)
    G, N, D = x.shape
    NB, KB = N // P, D // P
    xT = np.ascontiguousarray(x.reshape(G, P, NB, KB, P).transpose(0, 4, 3, 2, 1)).reshape(G, P, KB, N)
    adjT = np.ascontiguousarray(adj.reshape(G, P, NB, P, NB).transpose(0, 3, 4, 2, 1)).reshape(G, P, NB, N)
    arrays = {"xT": xT, "adjT": adjT, "x": x, "Wv": L0_gnn_Wv, "bv": L0_gnn_bv, "aw": L0_gnn_aw, "ab": L0_gnn_ab,
              "Wk": L0_gnn_Wk, "bk": L0_gnn_bk}
    arrays = {k: np.ascontiguousarray(a) for k, a in arrays.items()}
    nc = bacc.Bacc("TRN2", target_bir_lowering=False, num_devices=1)
    ins = [nc.dram_tensor(f"{k}_dram", a.shape, mybir.dt.from_np(a.dtype), kind="ExternalInput").ap()
           for k, a in arrays.items()]
    out = nc.dram_tensor("out_dram", x.shape, F32, kind="ExternalOutput").ap()
    build(nc, *ins, out)
    r = run_bass_kernel_spmd(nc, [{f"{k}_dram": a for k, a in arrays.items()}], core_ids=[0])
    return r.results[0]["out_dram"]
```

```python
from contextlib import ExitStack

import concourse.bass as bass
from concourse import mybir

ALU = mybir.AluOpType
ACT = mybir.ActivationFunctionType
F32 = mybir.dt.float32
F32R = mybir.dt.float32r

P = 128
ROWSUM_EPS = 1e-12
LN_EPS = 1e-5
PAR = 2


def build(nc, xT, adjT, x, Wv, bv, aw, ab, Wk, bk, out):
    G, N, D = x.shape
    NB = N // P
    KB = D // P
    STEPS = Wk.shape[0]
    assert NB == 4 and KB == 2 and STEPS == 3 and G % 2 == 0
    WA = 2 * D
    WB = D + 2
    SJ, SI = D, D + 1
    U1 = D + 2
    PAIR = NB // 2

    xT_of = xT.rearrange("(q u) p k n -> q u p k n", u=PAR)
    adjT_of = adjT.rearrange("(q u) p b n -> q u p b n", u=PAR)
    x_of = x.rearrange("(q u) (p b) d -> q u p (b d)", u=PAR, b=NB)
    out_of = out.rearrange("(q u) (p b) d -> q u p (b d)", u=PAR, b=NB)

    def done(g4, n):
        return g4 + n

    with ExitStack() as ctx:
        def sb(name, shape, dt=F32):
            return ctx.enter_context(nc.sbuf_tensor(name, shape, dt))

        def ps(name, shape):
            return ctx.enter_context(nc.psum_tensor(name, shape, F32))

        def sem(name):
            return ctx.enter_context(nc.semaphore(name))

        w_raw = sb("w_raw", [P, KB, WA + WB])
        w_hi = sb("w_hi", [P, KB, WA + WB], F32R)
        w_lo = sb("w_lo", [P, KB, WA + WB], F32R)
        wv = sb("wv", [P, KB, D])
        aw_row = sb("aw_row", [P, 2, D])
        bv_row = sb("bv_row", [P, D])
        bk_row = sb("bk_row", [P, STEPS, D])
        ab_col = sb("ab_col", [P, 1])
        aw_sum = sb("aw_sum", [P, D])
        b01_row = sb("b01_row", [P, D])
        product = sb("product", [P, 5, D])
        c_col = sb("c_col", [P, 1])
        bias_row = sb("bias_row", [P, WB])
        ident = sb("ident", [P, P])
        xT_in = [sb(f"xT_in{u}", [P, KB, N]) for u in range(PAR)]
        adj_in = [sb(f"adj_in{u}", [P, NB, N]) for u in range(PAR)]
        x_in = [sb(f"x_in{u}", [P, NB, D]) for u in range(PAR)]
        xT_hi = [sb(f"xT_hi{u}", [P, KB, N], F32R) for u in range(PAR)]
        xT_lo = [sb(f"xT_lo{u}", [P, KB, N], F32R) for u in range(PAR)]
        g0s = [sb(f"g0s{u}", [P, NB, WB]) for u in range(PAR)]
        g1 = [sb(f"g1_{u}", [P, NB, D]) for u in range(PAR)]
        factors = [sb(f"factors{u}", [P, NB, 2]) for u in range(PAR)]
        g2_hi = [sb(f"g2_hi{u}", [P, NB, U1], F32R) for u in range(PAR)]
        g2_lo = [sb(f"g2_lo{u}", [P, NB, U1], F32R) for u in range(PAR)]
        alpha = sb("alpha", [P, NB, N])
        al_hi = [sb(f"al_hi{u}", [P, NB, N], F32R) for u in range(PAR)]
        al_lo = [sb(f"al_lo{u}", [P, NB, N], F32R) for u in range(PAR)]
        denom = sb("denom", [P, NB])
        rcp = [sb(f"rcp{u}", [P, NB]) for u in range(PAR)]
        rcp_f = sb("rcp_f", [P, NB])
        v = sb("v", [P, NB, D])
        v_hi = sb("v_hi", [P, NB, D], F32R)
        v_lo = sb("v_lo", [P, NB, D], F32R)
        h = sb("h", [P, NB, D])
        y = [sb(f"y{u}", [P, NB, D]) for u in range(PAR)]
        y_sum = sb("y_sum", [P, NB])
        warm = sb("warm", [P, 1])
        dev_sum = sb("dev_sum", [P, NB])
        minus_half = sb("minus_half", [P, PAIR])
        var_eps = sb("var_eps", [P, NB])
        minus_mean = sb("minus_mean", [P, NB])
        rstd = sb("rstd", [P, NB])
        shift = sb("shift", [P, NB])
        res = [sb(f"res{u}", [P, NB, D]) for u in range(PAR)]
        ps_a = ps("ps_a", [P, 2, WA])
        ps_b = ps("ps_b", [P, 512])
        ps_z = ps("ps_z", [P, N])
        ps_u = ps("ps_u", [P, NB, 512])

        w_loaded = sem("w_loaded")
        w12_loaded = sem("w12_loaded")
        v_loaded = sem("v_loaded")
        rows_loaded = sem("rows_loaded")
        xT_loaded = [sem(f"xT_loaded{u}") for u in range(PAR)]
        adj_loaded = [sem(f"adj_loaded{u}") for u in range(PAR)]
        x_loaded = [sem(f"x_loaded{u}") for u in range(PAR)]
        stored = [sem(f"stored{u}") for u in range(PAR)]
        zeroed = sem("zeroed")
        ident_ready = sem("ident_ready")
        setup = sem("setup")
        w_hi_ready = sem("w_hi_ready")
        w_ready = sem("w_ready")
        xh_ready = sem("xh_ready")
        x_split = sem("x_split")
        wa_done = sem("wa_done")
        wb_done = sem("wb_done")
        g1_ready = sem("g1_ready")
        g2_ready = sem("g2_ready")
        g0s_ready = sem("g0s_ready")
        z_done = sem("z_done")
        factors_done = sem("factors_done")
        fh_ready = sem("fh_ready")
        f_ready = sem("f_ready")
        rcpf_done = sem("rcpf_done")
        exp_done = sem("exp_done")
        alpha_done = sem("alpha_done")
        alh_ready = sem("alh_ready")
        al_ready = sem("al_ready")
        t1_done = sem("t1_done")
        denom_done = sem("denom_done")
        rcp_done = sem("rcp_done")
        v_done = sem("v_done")
        vh_ready = sem("vh_ready")
        v_ready = sem("v_ready")
        t2_done = sem("t2_done")
        h_done = sem("h_done")
        y_done = sem("y_done")
        mean_done = sem("mean_done")
        dev_done = sem("dev_done")
        eps_done = sem("eps_done")
        rstd_done = sem("rstd_done")
        norm_ready = sem("norm_ready")
        res_ready = sem("res_ready")
        last_half = sem("last_half")

        block = ctx.enter_context(nc.Block())

        LOOPED = 4 * (G - 2)

        @block.sync
        def _(sp):
            def load_xT(q, u, first=False):
                if not first:
                    sp.wait_ge(x_split, done(8 * q + 4 * u, -4))
                sp.dma_start(xT_in[u][:, :, :], xT_of[q, u]).then_inc(xT_loaded[u], 16)

            def load_adj(q, u, first=False):
                if not first:
                    sp.wait_ge(alpha_done, done(8 * q + 4 * u, -4))
                sp.dma_start(adj_in[u][:, :, :], adjT_of[q, u]).then_inc(adj_loaded[u], 16)

            def load_x(q, u, first=False):
                if not first:
                    sp.wait_ge(y_done, done(8 * q + 4 * u, -4))
                sp.dma_start(x_in[u][:, :, :].rearrange("p b d -> p (b d)"), x_of[q, u]).then_inc(x_loaded[u], 16)

            sp.dma_start(wv[:, :, :], Wv.rearrange("(k p) n -> p k n", p=P)).then_inc(v_loaded, 16)
            sp.dma_start(w_raw[:, :, WA:WA + D], Wk[0].rearrange("(k p) n -> p k n", p=P)).then_inc(w_loaded, 16)
            sp.dma_start(bv_row[:, :], bv.partition_broadcast(P)).then_inc(rows_loaded, 16)
            sp.dma_start(ab_col[:, :], ab.partition_broadcast(P)).then_inc(rows_loaded, 16)
            sp.dma_start(bk_row[:, :, :], bk.partition_broadcast(P)).then_inc(rows_loaded, 16)
            for k in range(1, STEPS):
                sp.dma_start(w_raw[:, :, (k - 1) * D:k * D], Wk[k].rearrange("(k p) n -> p k n", p=P))\
                    .then_inc(w12_loaded, 16)
            load_xT(0, 1, first=True)
            load_adj(0, 0, first=True)
            load_adj(0, 1, first=True)
            for u in range(PAR):
                load_xT(1, u)
                load_adj(1, u)
                load_x(0, u, first=True)
            with sp.Fori(2, G // PAR, 1) as q:
                for u in range(PAR):
                    load_xT(q, u)
                    load_adj(q, u)
                    load_x(q - 1, u)
            for u in range(PAR):
                load_x(G // PAR - 1, u)

        @block.gpsimd
        def _(pool):
            nc.gpsimd.memset(ident[:, :], 0.0).then_inc(zeroed, 1)
            pool.wait_ge(zeroed, 1)
            nc.gpsimd.affine_select(out=ident[:, :], in_=ident[:, :], compare_op=ALU.not_equal, fill=1.0, base=0,
                                    pattern=[[-1, P]], channel_multiplier=1).then_inc(ident_ready, 1)
            nc.gpsimd.memset(minus_half[:, :], -0.5).then_inc(zeroed, 1)
            pool.wait_ge(zeroed, 2)

            def mean(g4, half):
                rows = slice(2 * half, 2 * half + 2)
                pool.wait_ge(y_done, done(g4, 2 * half + 2))
                nc.gpsimd.tensor_scalar(minus_mean[:, rows], y_sum[:, rows], -1.0 / D, None, ALU.mult)\
                    .then_inc(mean_done, 2)

            def norm(g4, half):
                rows = slice(2 * half, 2 * half + 2)
                n = done(g4, 2 * half + 2)
                pool.wait_ge(dev_done, n)
                nc.gpsimd.tensor_scalar(var_eps[:, rows], dev_sum[:, rows], 1.0 / D, LN_EPS, ALU.mult, ALU.add)\
                    .then_inc(eps_done, 2)
                if half == 0 and (not isinstance(g4, int) or g4 > 0):
                    pool.wait_ge(res_ready, g4)
                pool.wait_ge(eps_done, n)
                nc.gpsimd.tensor_tensor(rstd[:, rows], var_eps[:, rows], minus_half[:, :], ALU.pow)\
                    .then_inc(rstd_done, 2)
                pool.wait_ge(mean_done, n)
                pool.wait_ge(rstd_done, n)
                nc.gpsimd.tensor_tensor(shift[:, rows], minus_mean[:, rows], rstd[:, rows], ALU.mult)\
                    .then_inc(norm_ready, 2)

            def both(g4):
                mean(g4, 0)
                mean(g4, 1)
                norm(g4, 0)
                norm(g4, 1)

            both(0)
            with pool.Fori(4, 4 * G, 4) as g4:
                both(g4)

        @block.tensor
        def _(pe):
            def products_a(g4, u, blocks):
                for b in blocks:
                    if b >= 2 or not isinstance(g4, int) or g4 >= 4:
                        pe.wait_ge(g2_ready, done(g4, b - 1))
                    rows = slice(b * P, (b + 1) * P)
                    for k in range(KB):
                        bank = ps_a[:, b % 2, :]
                        nc.tensor.matmul(bank, xT_hi[u][:, k, rows], w_hi[:, k, 0:WA], start=k == 0, stop=False)
                        nc.tensor.matmul(bank, xT_hi[u][:, k, rows], w_lo[:, k, 0:WA], start=False, stop=False)
                        last = nc.tensor.matmul(bank, xT_lo[u][:, k, rows], w_hi[:, k, 0:WA], start=False,
                                                stop=k == KB - 1)
                    last.then_inc(wa_done, 1)

            def products_b(g4, u, b, start=False):
                if b == 0:
                    pe.wait_ge(x_split, done(g4, 4))
                if not start:
                    pe.wait_ge(g0s_ready, done(g4, b))
                elif g4 > 0:
                    pe.wait_ge(g0s_ready, done(g4, b - 3))
                rows = slice(b * P, (b + 1) * P)
                bank = ps_u[:, b, 0:WB] if start else ps_b[:, 0:WB]
                for k in range(KB):
                    cols = slice(WA, WA + WB)
                    nc.tensor.matmul(bank, xT_hi[u][:, k, rows], w_hi[:, k, cols], start=k == 0, stop=False)
                    nc.tensor.matmul(bank, xT_hi[u][:, k, rows], w_lo[:, k, cols], start=False, stop=False)
                    last = nc.tensor.matmul(bank, xT_lo[u][:, k, rows], w_hi[:, k, cols], start=False,
                                            stop=k == KB - 1)
                last.then_inc(wb_done, 1)

            def spread_si(g4, u):
                pe.wait_ge(g0s_ready, done(g4, 4))
                if not isinstance(g4, int) or g4 > 0:
                    pe.wait_ge(exp_done, g4)
                for b in range(NB):
                    last = nc.tensor.transpose(ps_z[:, b * P:(b + 1) * P],
                                               g0s[u][:, b, SI:SI + 1].to_broadcast([P, P]), ident[:, :])
                last.then_inc(z_done, 4)

            def apply_1(g4, u, b):
                if b == 0:
                    pe.wait_ge(al_ready, done(g4, 4))
                    pe.wait_ge(g2_ready, done(g4, 4))
                    pe.wait_ge(f_ready, done(g4, 4))
                if not isinstance(g4, int) or g4 > 0:
                    pe.wait_ge(h_done, done(g4, b - 3))
                else:
                    pe.wait_ge(g0s_ready, done(4, b + 1))
                cols = slice(b * P, (b + 1) * P)
                for j in range(NB):
                    nc.tensor.matmul(ps_u[:, b, 0:U1], al_hi[u][:, j, cols], g2_hi[u][:, j, :], start=j == 0,
                                     stop=False)
                    nc.tensor.matmul(ps_u[:, b, 0:U1], al_hi[u][:, j, cols], g2_lo[u][:, j, :], start=False,
                                     stop=False)
                    last = nc.tensor.matmul(ps_u[:, b, 0:U1], al_lo[u][:, j, cols], g2_hi[u][:, j, :], start=False,
                                            stop=j == NB - 1)
                last.then_inc(t1_done, 1)

            def apply_2(g4, u, b, sources=range(NB)):
                pe.wait_ge(v_ready, done(g4, max(sources) + 1))
                if max(sources) < NB - 1:
                    pe.wait_ge(v_done, done(g4, b + 1))
                cols = slice(b * P, (b + 1) * P)
                for j in sources:
                    nc.tensor.matmul(ps_u[:, b, 0:D], al_hi[u][:, j, cols], v_hi[:, j, :], start=j == 0, stop=False)
                    nc.tensor.matmul(ps_u[:, b, 0:D], al_hi[u][:, j, cols], v_lo[:, j, :], start=False, stop=False)
                    last = nc.tensor.matmul(ps_u[:, b, 0:D], al_lo[u][:, j, cols], v_hi[:, j, :], start=False,
                                            stop=j == NB - 1)
                if NB - 1 in sources:
                    last.then_inc(t2_done, 1)

            ALL = range(NB)
            pe.wait_ge(w_ready, 1)
            for b in ALL:
                products_b(0, 0, b, start=True)
            pe.wait_ge(w_ready, 2)
            products_a(0, 0, [0])
            pe.wait_ge(ident_ready, 1)
            spread_si(0, 0)
            products_a(0, 0, ALL[1:])
            for b in ALL:
                products_b(4, 1, b, start=True)
            apply_1(0, 0, 0)
            spread_si(4, 1)
            apply_1(0, 0, 1)
            apply_1(0, 0, 2)
            products_a(4, 1, [0])
            apply_1(0, 0, 3)
            with pe.Fori(0, LOOPED, 8) as pair4:
                for u in range(PAR):
                    g4 = pair4 + 4 * u
                    products_a(g4 + 4, 1 - u, ALL[1:])
                    for b in ALL:
                        apply_2(g4, u, b)
                        products_b(g4 + 8, u, b)
                    apply_1(g4 + 4, 1 - u, 0)
                    spread_si(g4 + 8, u)
                    apply_1(g4 + 4, 1 - u, 1)
                    apply_1(g4 + 4, 1 - u, 2)
                    products_a(g4 + 8, u, [0])
                    apply_1(g4 + 4, 1 - u, 3)
            products_a(LOOPED + 4, 1, ALL[1:])
            for b in ALL:
                apply_2(LOOPED, 0, b)
            for b in ALL:
                apply_1(LOOPED + 4, 1, b)
            for sources in (ALL[:2], ALL[2:]):
                for b in ALL:
                    apply_2(LOOPED + 4, 1, b, sources)

        @block.scalar
        def _(act):
            def split_x(g4, u, loads):
                act.wait_ge(xT_loaded[u], loads)
                if not isinstance(g4, int) or g4 >= 8:
                    act.wait_ge(wa_done, done(g4, -4))
                nc.scalar.activation(xT_hi[u][:, :, :], xT_in[u][:, :, :], ACT.Copy).then_inc(xh_ready, 4)

            def leave_a(g4, u, b):
                act.wait_ge(wa_done, done(g4, b + 1))
                if b == 0 and (not isinstance(g4, int) or g4 >= 8):
                    act.wait_ge(t1_done, done(g4, -4))
                    act.wait_ge(v_done, done(g4, -4))
                f = factors[u][:, b, 0:1]
                nc.scalar.activation(g2_hi[u][:, b, 0:D], ps_a[:, b % 2, D:WA], ACT.Copy, scale=f)
                nc.scalar.activation(g1[u][:, b, :], ps_a[:, b % 2, 0:D], ACT.Copy, scale=f).then_inc(g1_ready, 1)

            def factor(g4, u):
                act.wait_ge(g0s_ready, done(g4, 4))
                if not isinstance(g4, int) or g4 >= 8:
                    act.wait_ge(v_done, done(g4, -4))
                nc.scalar.activation(factors[u][:, :, :], g0s[u][:, :, D:WB], ACT.Exp, scale=0.25)\
                    .then_inc(factors_done, 4)
                act.wait_ge(factors_done, done(g4, 4))
                nc.scalar.activation(g2_hi[u][:, :, D:U1], factors[u][:, :, :], ACT.Copy).then_inc(fh_ready, 4)

            def exponential(g4, u, b):
                if b == 0:
                    act.wait_ge(z_done, done(g4, 4))
                    if not isinstance(g4, int) or g4 > 0:
                        act.wait_ge(al_ready, g4)
                nc.scalar.activation(alpha[:, b, :], ps_z[:, :], ACT.Exp, scale=-1.0, bias=g0s[u][:, b, SJ:SJ + 1])\
                    .then_inc(exp_done, 1)

            def alpha_high(g4, u, half):
                act.wait_ge(alpha_done, done(g4, 2 * half + 2))
                if half == 0 and (not isinstance(g4, int) or g4 >= 8):
                    act.wait_ge(t2_done, done(g4, -4))
                rows = slice(2 * half, 2 * half + 2)
                nc.scalar.activation(al_hi[u][:, rows, :], alpha[:, rows, :], ACT.Copy).then_inc(alh_ready, 2)

            def v_high(g4, half):
                act.wait_ge(v_done, done(g4, 2 * half + 2))
                if half == 0 and (not isinstance(g4, int) or g4 > 0):
                    act.wait_ge(t2_done, g4)
                rows = slice(2 * half, 2 * half + 2)
                nc.scalar.activation(v_hi[:, rows, :], v[:, rows, :], ACT.Copy).then_inc(vh_ready, 2)

            def deviations(g4, u, half, stores=0):
                act.wait_ge(mean_done, done(g4, 2 * half + 2))
                if half == 0 and (not isinstance(g4, int) or g4 >= 8):
                    act.wait_ge(stored[u], stores)
                for b in range(2 * half, 2 * half + 2):
                    nc.scalar.activation(res[u][:, b, :], y[u][:, b, :], ACT.Square, bias=minus_mean[:, b:b + 1],
                                         accum_out=dev_sum[:, b:b + 1]).then_inc(dev_done, 1)

            def normalise(g4, u, half):
                act.wait_ge(norm_ready, done(g4, 2 * half + 2))
                for b in range(2 * half, 2 * half + 2):
                    nc.scalar.activation(res[u][:, b, :], y[u][:, b, :], ACT.Identity, bias=shift[:, b:b + 1],
                                         scale=rstd[:, b:b + 1]).then_inc(res_ready, 1)

            def store(q, g4, u):
                act.wait_ge(res_ready, done(g4, 4))
                act.dma_start(out_of[q, u], res[u][:, :, :].rearrange("p b d -> p (b d)")).then_inc(stored[u], 16)

            act.dma_start(aw_row[:, :, :].rearrange("p a d -> p (a d)"),
                          aw.rearrange("n a -> a n").partition_broadcast(P)).then_inc(v_loaded, 16)
            act.dma_start(xT_in[0][:, :, :], xT_of[0, 0]).then_inc(xT_loaded[0], 16)
            act.wait_ge(ident_ready, 1)
            nc.scalar.activation(warm[:, :], ident[:, 0:1], ACT.Exp)
            split_x(0, 0, 16)
            act.wait_ge(setup, 4)
            act.wait_ge(w_loaded, 16)
            nc.scalar.activation(w_hi[:, :, WA:], w_raw[:, :, WA:], ACT.Copy).then_inc(w_hi_ready, 1)
            act.wait_ge(w12_loaded, 32)
            nc.scalar.activation(w_hi[:, :, 0:WA], w_raw[:, :, 0:WA], ACT.Copy).then_inc(w_hi_ready, 1)
            split_x(4, 1, 16)
            factor(0, 0)
            exponential(0, 0, 0)
            exponential(0, 0, 1)
            leave_a(0, 0, 0)
            exponential(0, 0, 2)
            leave_a(0, 0, 1)
            exponential(0, 0, 3)
            leave_a(0, 0, 2)
            alpha_high(0, 0, 0)
            leave_a(0, 0, 3)
            alpha_high(0, 0, 1)
            factor(4, 1)
            for b in range(NB):
                exponential(4, 1, b)

            def step(q, g4, u, first=False, follow=2, xT_loads=0, stores=0):
                if follow >= 2:
                    split_x(g4 + 8, u, xT_loads)
                v_high(g4, 0)
                if follow >= 1:
                    leave_a(g4 + 4, 1 - u, 0)
                v_high(g4, 1)
                if follow >= 1:
                    for b in range(1, NB):
                        leave_a(g4 + 4, 1 - u, b)
                    alpha_high(g4 + 4, 1 - u, 0)
                    alpha_high(g4 + 4, 1 - u, 1)
                if not first:
                    deviations(g4 - 4, 1 - u, 1)
                    finish(q, g4 - 4, 1 - u)
                if follow >= 2:
                    factor(g4 + 8, u)
                    for b in range(NB):
                        exponential(g4 + 8, u, b)
                deviations(g4, u, 0, stores)

            def finish(q, g4, u):
                normalise(g4, u, 0)
                normalise(g4, u, 1)
                store(q, g4, u)

            LAST = G // PAR - 1
            step(0, 0, 0, first=True, xT_loads=32)
            step(0, 4, 1, xT_loads=32)
            with act.Fori(1, LAST, 1) as q:
                step(q - 1, 8 * q, 0, xT_loads=16 * q + 32, stores=16 * q)
                step(q, 8 * q + 4, 1, xT_loads=16 * q + 32, stores=16 * q)
            step(LAST - 1, LOOPED, 0, follow=1, stores=16 * LAST)
            step(LAST, LOOPED + 4, 1, follow=0, stores=16 * LAST)
            deviations(LOOPED + 4, 1, 1)
            for half in range(2):
                if half == 0:
                    normalise(LOOPED + 4, 1, 0)
                    act.wait_ge(res_ready, done(LOOPED + 4, 2))
                else:
                    act.wait_ge(last_half, PAIR)
                cols = slice(half * PAIR * D, (half + 1) * PAIR * D)
                act.dma_start(out_of[LAST, 1][:, cols], res[1][:, :, :].rearrange("p b d -> p (b d)")[:, cols])\
                    .then_inc(stored[1], 16)
            act.wait_ge(stored[0], 8 * G)
            act.wait_ge(stored[1], 8 * G + 16)

        @block.vector
        def _(dve):
            def split_x(g4, u):
                dve.wait_ge(xh_ready, done(g4, 4))
                nc.vector.tensor_tensor(xT_lo[u][:, :, :], xT_in[u][:, :, :], xT_hi[u][:, :, :].bitcast(F32),
                                        ALU.subtract).then_inc(x_split, 4)

            def leave_b(g4, u, b, start=False):
                dve.wait_ge(wb_done, done(g4, b + 1))
                if not isinstance(g4, int) or g4 >= 8:
                    dve.wait_ge(h_done, done(g4, b - 7))
                bank = ps_u[:, b, 0:WB] if start else ps_b[:, 0:WB]
                nc.vector.tensor_tensor(g0s[u][:, b, :], bank, bias_row[:, :], ALU.add)\
                    .then_inc(g0s_ready, 1)

            def g2_low(g4, u, b):
                dve.wait_ge(g1_ready, done(g4, b + 1))
                nc.vector.scalar_tensor_tensor(g2_lo[u][:, b, 0:D], ps_a[:, b % 2, D:WA], factors[u][:, b, 0:1],
                                               g2_hi[u][:, b, 0:D].bitcast(F32), ALU.mult, ALU.subtract)\
                    .then_inc(g2_ready, 1)

            def f_low(g4, u):
                dve.wait_ge(fh_ready, done(g4, 4))
                nc.vector.tensor_tensor(g2_lo[u][:, :, D:U1], factors[u][:, :, :],
                                        g2_hi[u][:, :, D:U1].bitcast(F32), ALU.subtract).then_inc(f_ready, 4)

            def times_adj(g4, u, half, loads=0):
                dve.wait_ge(exp_done, done(g4, 2 * half + 2))
                if half == 0:
                    dve.wait_ge(adj_loaded[u], loads)
                two = alpha[:, 2 * half:2 * half + 2, :]
                nc.vector.scalar_tensor_tensor(two, two, 1.0, adj_in[u][:, 2 * half:2 * half + 2, :], ALU.max,
                                               ALU.mult)\
                    .then_inc(alpha_done, 2)

            def alpha_low(g4, u, half):
                dve.wait_ge(alh_ready, done(g4, 2 * half + 2))
                rows = slice(2 * half, 2 * half + 2)
                nc.vector.tensor_tensor(al_lo[u][:, rows, :], alpha[:, rows, :], al_hi[u][:, rows, :].bitcast(F32),
                                        ALU.subtract).then_inc(al_ready, 2)

            def row_sums(g4, u, half):
                rows = slice(2 * half, 2 * half + 2)
                dve.wait_ge(t1_done, done(g4, 2 * half + 2))
                nc.vector.scalar_tensor_tensor(denom[:, rows], factors[u][:, rows, 1], ROWSUM_EPS, ps_u[:, rows, D],
                                               ALU.mult, ALU.add).then_inc(denom_done, 2)

            def invert(g4, u, half):
                rows = slice(2 * half, 2 * half + 2)
                dve.wait_ge(denom_done, done(g4, 2 * half + 2))
                nc.vector.reciprocal(rcp[u][:, rows], denom[:, rows]).then_inc(rcp_done, 2)

            def invert_f(g4, u, half):
                rows = slice(2 * half, 2 * half + 2)
                dve.wait_ge(rcp_done, done(g4, 2 * half + 2))
                nc.vector.tensor_tensor(rcp_f[:, rows], rcp[u][:, rows], factors[u][:, rows, 0], ALU.mult)\
                    .then_inc(rcpf_done, 2)

            def combine(g4, u, half):
                dve.wait_ge(rcpf_done, done(g4, 2 * half + 2))
                for b in range(2 * half, 2 * half + 2):
                    nc.vector.scalar_tensor_tensor(v[:, b, :], ps_u[:, b, 0:D], rcp_f[:, b:b + 1], g1[u][:, b, :],
                                                   ALU.mult, ALU.add).then_inc(v_done, 1)

            def v_low(g4, half):
                dve.wait_ge(vh_ready, done(g4, 2 * half + 2))
                rows = slice(2 * half, 2 * half + 2)
                nc.vector.tensor_tensor(v_lo[:, rows, :], v[:, rows, :], v_hi[:, rows, :].bitcast(F32),
                                        ALU.subtract).then_inc(v_ready, 2)

            def hidden(g4, u, b):
                dve.wait_ge(t2_done, done(g4, b + 1))
                nc.vector.scalar_tensor_tensor(h[:, b, :], ps_u[:, b, 0:D], rcp[u][:, b:b + 1], g0s[u][:, b, 0:D],
                                               ALU.mult, ALU.add).then_inc(h_done, 1)

            def residual(g4, u, b, loads):
                dve.wait_ge(h_done, done(g4, b + 1))
                if b == 0:
                    dve.wait_ge(x_loaded[u], loads)
                    if not isinstance(g4, int) or g4 > 0:
                        dve.wait_ge(norm_ready, g4)
                    if not isinstance(g4, int) or g4 >= 8:
                        dve.wait_ge(res_ready, done(g4, -4))
                nc.vector.scalar_tensor_tensor(y[u][:, b, :], h[:, b, :], 0.0, x_in[u][:, b, :], ALU.max, ALU.add,
                                               accum_out=y_sum[:, b:b + 1]).then_inc(y_done, 1)

            nc.vector.memset(bias_row[:, SI:SI + 1], 0.0)
            dve.wait_ge(v_loaded, 32)
            for k in range(KB):
                for a in range(2):
                    nc.vector.tensor_tensor_reduce(out=product[:, 2 * k + a, :], in0=wv[:, k, :], in1=aw_row[:, a, :],
                                                   scale=0.8 if a == 0 else -0.8, scalar=0.0, op0=ALU.mult, op1=ALU.add,
                                                   accum_out=w_raw[:, k, WA + D + a:WA + D + a + 1])\
                        .then_inc(setup, 1)
            split_x(0, 0)
            dve.wait_ge(w_hi_ready, 1)
            nc.vector.tensor_tensor(w_lo[:, :, WA:], w_raw[:, :, WA:], w_hi[:, :, WA:].bitcast(F32), ALU.subtract)\
                .then_inc(w_ready, 1)
            dve.wait_ge(rows_loaded, 48)
            nc.vector.tensor_tensor(aw_sum[:, :], aw_row[:, 0, :], aw_row[:, 1, :], ALU.add).then_inc(setup, 1)
            nc.vector.tensor_tensor(b01_row[:, :], bk_row[:, 0, :], bk_row[:, 1, :], ALU.add).then_inc(setup, 1)
            dve.wait_ge(setup, 6)
            nc.vector.tensor_tensor_reduce(out=product[:, 4, :], in0=bv_row[:, :], in1=aw_sum[:, :], scale=0.8,
                                           scalar=0.0, op0=ALU.mult, op1=ALU.add, accum_out=c_col[:, :])\
                .then_inc(setup, 1)
            nc.vector.tensor_tensor(bias_row[:, 0:D], b01_row[:, :], bk_row[:, 2, :], ALU.add).then_inc(setup, 1)
            dve.wait_ge(setup, 8)
            nc.vector.scalar_tensor_tensor(bias_row[:, SJ:SJ + 1], ab_col[:, :], 0.8, c_col[:, :], ALU.mult, ALU.add)\
                .then_inc(setup, 1)
            dve.wait_ge(setup, 9)
            leave_b(0, 0, 0, start=True)
            dve.wait_ge(w_hi_ready, 2)
            nc.vector.tensor_tensor(w_lo[:, :, 0:WA], w_raw[:, :, 0:WA], w_hi[:, :, 0:WA].bitcast(F32), ALU.subtract)\
                .then_inc(w_ready, 1)
            for b in range(1, NB):
                leave_b(0, 0, b, start=True)
            f_low(0, 0)
            split_x(4, 1)
            g2_low(0, 0, 0)
            times_adj(0, 0, 0, 16)
            g2_low(0, 0, 1)
            times_adj(0, 0, 1)
            g2_low(0, 0, 2)
            alpha_low(0, 0, 0)
            g2_low(0, 0, 3)
            alpha_low(0, 0, 1)
            for b in range(NB):
                leave_b(4, 1, b, start=True)
            times_adj(4, 1, 0, 16)
            row_sums(0, 0, 0)
            invert(0, 0, 0)
            invert_f(0, 0, 0)
            combine(0, 0, 0)

            def step(g4, u, follow=2, x_loads=8 * G, adj_loads=8 * G):
                if follow >= 1:
                    f_low(g4 + 4, 1 - u)
                row_sums(g4, u, 1)
                invert(g4, u, 1)
                invert_f(g4, u, 1)
                combine(g4, u, 1)
                if follow >= 1:
                    g2_low(g4 + 4, 1 - u, 0)
                v_low(g4, 0)
                v_low(g4, 1)
                if follow >= 1:
                    g2_low(g4 + 4, 1 - u, 1)
                    times_adj(g4 + 4, 1 - u, 1)
                    g2_low(g4 + 4, 1 - u, 2)
                if follow >= 2:
                    split_x(g4 + 8, u)
                if follow >= 1:
                    g2_low(g4 + 4, 1 - u, 3)
                hidden(g4, u, 0)
                if follow >= 2:
                    leave_b(g4 + 8, u, 0)
                if follow >= 1:
                    alpha_low(g4 + 4, 1 - u, 0)
                hidden(g4, u, 1)
                if follow >= 2:
                    leave_b(g4 + 8, u, 1)
                if follow >= 1:
                    alpha_low(g4 + 4, 1 - u, 1)
                hidden(g4, u, 2)
                residual(g4, u, 0, x_loads)
                if follow >= 2:
                    leave_b(g4 + 8, u, 2)
                residual(g4, u, 1, x_loads)
                hidden(g4, u, 3)
                residual(g4, u, 2, x_loads)
                if follow >= 2:
                    leave_b(g4 + 8, u, 3)
                residual(g4, u, 3, x_loads)
                if follow >= 2:
                    times_adj(g4 + 8, u, 0, adj_loads)
                if follow >= 1:
                    row_sums(g4 + 4, 1 - u, 0)
                    invert(g4 + 4, 1 - u, 0)
                    invert_f(g4 + 4, 1 - u, 0)
                    combine(g4 + 4, 1 - u, 0)

            step(0, 0, x_loads=16, adj_loads=32)
            step(4, 1, x_loads=16, adj_loads=32)
            with dve.Fori(8, LOOPED, 8) as pair4:
                for u in range(PAR):
                    step(pair4 + 4 * u, u, x_loads=2 * pair4 + 16, adj_loads=2 * pair4 + 32)
            step(LOOPED, 0, follow=1)
            step(LOOPED + 4, 1, follow=0)
            dve.wait_ge(norm_ready, 4 * G)
            for b in range(PAIR, NB):
                nc.vector.tensor_scalar(res[1][:, b, :], y[1][:, b, :], rstd[:, b:b + 1], shift[:, b:b + 1],
                                        ALU.mult, ALU.add).then_inc(last_half, 1)


def kernel(x, adj, L0_gnn_Wv, L0_gnn_bv, L0_gnn_aw, L0_gnn_ab, L0_gnn_Wk, L0_gnn_bk):
    import numpy as np
    import concourse.bacc as bacc
    from concourse.bass_utils import run_bass_kernel_spmd

    x, adj = np.asarray(x), np.asarray(adj)
    G, N, D = x.shape
    NB, KB = N // P, D // P
    xT = np.ascontiguousarray(x.reshape(G, P, NB, KB, P).transpose(0, 4, 3, 2, 1)).reshape(G, P, KB, N)
    adjT = np.ascontiguousarray(adj.reshape(G, P, NB, P, NB).transpose(0, 3, 4, 2, 1)).reshape(G, P, NB, N)
    arrays = {"xT": xT, "adjT": adjT, "x": x, "Wv": L0_gnn_Wv, "bv": L0_gnn_bv, "aw": L0_gnn_aw, "ab": L0_gnn_ab,
              "Wk": L0_gnn_Wk, "bk": L0_gnn_bk}
    arrays = {k: np.ascontiguousarray(a) for k, a in arrays.items()}
    nc = bacc.Bacc("TRN2", target_bir_lowering=False, num_devices=1)
    ins = [nc.dram_tensor(f"{k}_dram", a.shape, mybir.dt.from_np(a.dtype), kind="ExternalInput").ap()
           for k, a in arrays.items()]
    out = nc.dram_tensor("out_dram", x.shape, F32, kind="ExternalOutput").ap()
    build(nc, *ins, out)
    r = run_bass_kernel_spmd(nc, [{f"{k}_dram": a for k, a in arrays.items()}], core_ids=[0])
    return r.results[0]["out_dram"]
```

```python
from contextlib import ExitStack

import concourse.bass as bass
from concourse import mybir

ALU = mybir.AluOpType
ACT = mybir.ActivationFunctionType
F32 = mybir.dt.float32
F32R = mybir.dt.float32r

P = 128
ROWSUM_EPS = 1e-12
LN_EPS = 1e-5
PAR = 2
WARM_UP = 4, 5


def build(nc, xT, adjT, x, WvT, a_bv, ab, Wk, bk, out):
    G, N, D = x.shape
    NB = N // P
    KB = D // P
    STEPS = Wk.shape[0]
    assert NB == 4 and KB == 2 and STEPS == 3 and G % 2 == 0
    WA = 2 * D
    WB = D + 2
    SJ, SI = D, D + 1
    U1 = D + 2
    PAIR = NB // 2
    HALF = N // 2

    xT_of = xT.rearrange("(q u) p k n -> q u p k n", u=PAR)
    adjT_of = adjT.rearrange("(q u) p b n -> q u p b n", u=PAR)
    x_of = x.rearrange("(q u) (p b) d -> q u p (b d)", u=PAR, b=NB)
    out_of = out.rearrange("(q u) (p b) d -> q u p (b d)", u=PAR, b=NB)

    def done(g4, n):
        return g4 + n

    with ExitStack() as ctx:
        def sb(name, shape, dt=F32):
            return ctx.enter_context(nc.sbuf_tensor(name, shape, dt))

        def ps(name, shape):
            return ctx.enter_context(nc.psum_tensor(name, shape, F32))

        def sem(name):
            return ctx.enter_context(nc.semaphore(name))

        w_raw = sb("w_raw", [P, KB, WA + WB])
        w_hi = sb("w_hi", [P, KB, WA + WB], F32R)
        w_lo = sb("w_lo", [P, KB, WA + WB], F32R)
        wvT = sb("wvT", [P, KB, D])
        a_bv_sb = sb("a_bv_sb", [P, KB, 3])
        bk_ab = sb("bk_ab", [STEPS, D + 2])
        c_col = sb("c_col", [P, 1])
        ones = sb("ones", [P, P])
        bias_row = sb("bias_row", [P, WB])
        ident = sb("ident", [P, P])
        xT_in = [sb(f"xT_in{u}", [P, KB, N]) for u in range(PAR)]
        adj_in = [sb(f"adj_in{u}", [P, NB, N]) for u in range(PAR)]
        x_in = [sb(f"x_in{u}", [P, NB, D]) for u in range(PAR)]
        xT_hi = [sb(f"xT_hi{u}", [P, KB, N], F32R) for u in range(PAR)]
        xT_lo = [sb(f"xT_lo{u}", [P, KB, N], F32R) for u in range(PAR)]
        g0s = [sb(f"g0s{u}", [P, NB, WB]) for u in range(PAR)]
        g1 = [sb(f"g1_{u}", [P, NB, D]) for u in range(PAR)]
        factors = [sb(f"factors{u}", [P, NB, 2]) for u in range(PAR)]
        g2_hi = [sb(f"g2_hi{u}", [P, NB, U1], F32R) for u in range(PAR)]
        g2_lo = [sb(f"g2_lo{u}", [P, NB, U1], F32R) for u in range(PAR)]
        alpha = sb("alpha", [P, NB, N])
        al_hi = [sb(f"al_hi{u}", [P, NB, N], F32R) for u in range(PAR)]
        al_lo = [sb(f"al_lo{u}", [P, NB, N], F32R) for u in range(PAR)]
        denom = sb("denom", [P, NB])
        rcp = [sb(f"rcp{u}", [P, NB]) for u in range(PAR)]
        rcp_f = sb("rcp_f", [P, NB])
        v = [sb(f"v{u}", [P, NB, D]) for u in range(PAR)]
        v_hi = [sb(f"v_hi{u}", [P, NB, D], F32R) for u in range(PAR)]
        v_lo = [sb(f"v_lo{u}", [P, NB, D], F32R) for u in range(PAR)]
        h = sb("h", [P, NB, D])
        y = [sb(f"y{u}", [P, NB, D]) for u in range(PAR)]
        y_sum = sb("y_sum", [P, NB])
        warm = sb("warm", [P, 1])
        dev_sum = sb("dev_sum", [P, NB])
        minus_half = sb("minus_half", [P, PAIR])
        var_eps = sb("var_eps", [P, NB])
        minus_mean = sb("minus_mean", [P, NB])
        rstd = sb("rstd", [P, NB])
        shift = sb("shift", [P, NB])
        res = [sb(f"res{u}", [P, NB, D]) for u in range(PAR)]
        ps_a = ps("ps_a", [P, 2, WA])
        ps_b = ps("ps_b", [P, 512])
        ps_z = ps("ps_z", [P, N])
        ps_u = ps("ps_u", [P, NB, 512])

        w_loaded = sem("w_loaded")
        w12_loaded = sem("w12_loaded")
        v_loaded = sem("v_loaded")
        x0_loaded = sem("x0_loaded")
        rows_loaded = sem("rows_loaded")
        xT_loaded = [sem(f"xT_loaded{u}") for u in range(PAR)]
        adj_loaded = [sem(f"adj_loaded{u}") for u in range(PAR)]
        x_loaded = [sem(f"x_loaded{u}") for u in range(PAR)]
        stored = [sem(f"stored{u}") for u in range(PAR)]
        zeroed = sem("zeroed")
        ident_ready = sem("ident_ready")
        score_done = sem("score_done")
        bias_done = sem("bias_done")
        setup = sem("setup")
        w_hi_ready = sem("w_hi_ready")
        w_ready = sem("w_ready")
        xh_ready = sem("xh_ready")
        x_split = sem("x_split")
        wa_done = sem("wa_done")
        wb_done = sem("wb_done")
        g1_ready = sem("g1_ready")
        g2_ready = sem("g2_ready")
        g0s_ready = sem("g0s_ready")
        z_done = sem("z_done")
        factors_done = sem("factors_done")
        fh_ready = sem("fh_ready")
        f_ready = sem("f_ready")
        rcpf_done = sem("rcpf_done")
        exp_done = sem("exp_done")
        alpha_done = sem("alpha_done")
        alh_ready = sem("alh_ready")
        al_ready = sem("al_ready")
        t1_done = sem("t1_done")
        denom_done = sem("denom_done")
        rcp_done = sem("rcp_done")
        v_done = sem("v_done")
        vh_ready = sem("vh_ready")
        v_ready = sem("v_ready")
        t2_done = sem("t2_done")
        h_done = sem("h_done")
        y_done = sem("y_done")
        mean_done = sem("mean_done")
        dev_done = sem("dev_done")
        eps_done = sem("eps_done")
        rstd_done = sem("rstd_done")
        norm_ready = sem("norm_ready")
        res_ready = sem("res_ready")
        last_block = sem("last_block")
        last_stored = sem("last_stored")

        block = ctx.enter_context(nc.Block())

        LOOPED = 4 * (G - 2)

        @block.sync
        def _(sp):
            def load_xT(q, u, first=False):
                if not first:
                    sp.wait_ge(x_split, done(8 * q + 4 * u, -4))
                sp.dma_start(xT_in[u][:, :, :], xT_of[q, u]).then_inc(xT_loaded[u], 16)

            def load_adj(q, u, first=False):
                if not first:
                    sp.wait_ge(alpha_done, done(8 * q + 4 * u, -4))
                sp.dma_start(adj_in[u][:, :, :], adjT_of[q, u]).then_inc(adj_loaded[u], 16)

            def load_x(q, u, first=False):
                if not first:
                    sp.wait_ge(y_done, done(8 * q + 4 * u, -4))
                sp.dma_start(x_in[u][:, :, :].rearrange("p b d -> p (b d)"), x_of[q, u]).then_inc(x_loaded[u], 16)

            sp.dma_start(wvT[:, :, :], WvT).then_inc(v_loaded, 16)
            sp.dma_start(w_raw[:, :, WA:WA + D], Wk[0].rearrange("(k p) n -> p k n", p=P)).then_inc(w_loaded, 16)
            sp.dma_start(bk_ab[:, 0:D], bk).then_inc(rows_loaded, 16)
            sp.wait_ge(zeroed, 1)
            sp.dma_start(bk_ab[0:1, D:D + 1], ab.rearrange("(o n) -> o n", o=1)).then_inc(rows_loaded, 16)
            for k in range(1, STEPS):
                sp.dma_start(w_raw[:, :, (k - 1) * D:k * D], Wk[k].rearrange("(k p) n -> p k n", p=P))\
                    .then_inc(w12_loaded, 16)
            load_xT(0, 1, first=True)
            load_adj(0, 0, first=True)
            load_adj(0, 1, first=True)
            for u in range(PAR):
                load_xT(1, u)
                load_adj(1, u)
                load_x(0, u, first=True)
            with sp.Fori(2, G // PAR, 1) as q:
                for u in range(PAR):
                    load_xT(q, u)
                    load_adj(q, u)
                    load_x(q - 1, u)
            for u in range(PAR):
                load_x(G // PAR - 1, u)

            results = [r[:, :, :].rearrange("p b d -> p (b d)") for r in res]
            sp.wait_ge(res_ready, 4 * G - 4)
            sp.dma_start(out_of[G // PAR - 1, 0], results[0]).then_inc(last_stored, 16)
            sp.wait_ge(res_ready, 4 * G - 2)
            sp.dma_start(out_of[G // PAR - 1, 1][:, 0:PAIR * D], results[1][:, 0:PAIR * D]).then_inc(last_stored, 16)
            sp.wait_ge(res_ready, 4 * G - 1)
            sp.wait_ge(last_block, 1)
            sp.dma_start(out_of[G // PAR - 1, 1][:, PAIR * D:], results[1][:, PAIR * D:]).then_inc(last_stored, 16)
            sp.wait_ge(stored[0], 8 * G - 16)
            sp.wait_ge(stored[1], 8 * G - 16)
            sp.wait_ge(last_stored, 48)

        @block.gpsimd
        def _(pool):
            nc.gpsimd.memset(bk_ab[:, D:D + 2], 0.0).then_inc(zeroed, 1)
            nc.gpsimd.memset(ident[:, :], 0.0).then_inc(zeroed, 1)
            nc.gpsimd.memset(ones[:, :], 1.0)
            pool.wait_ge(zeroed, 2)
            nc.gpsimd.affine_select(out=ident[:, :], in_=ident[:, :], compare_op=ALU.not_equal, fill=1.0, base=0,
                                    pattern=[[-1, P]], channel_multiplier=1).then_inc(ident_ready, 1)
            nc.gpsimd.memset(minus_half[:, :], -0.5).then_inc(zeroed, 1)
            pool.wait_ge(zeroed, 3)

            for g4, u in ((4, 1), (8, 0)):
                pool.wait_ge(xh_ready, done(g4, 4))
                pool.wait_ge(x_split, g4)
                if g4 >= 8:
                    pool.wait_ge(wa_done, done(g4, -4))
                nc.gpsimd.tensor_tensor(xT_lo[u][:, :, :], xT_in[u][:, :, :], xT_hi[u][:, :, :].bitcast(F32),
                                        ALU.subtract).then_inc(x_split, 4)

            def mean(g4, half):
                rows = slice(2 * half, 2 * half + 2)
                pool.wait_ge(y_done, done(g4, 2 * half + 2))
                if half == 0 and (not isinstance(g4, int) or g4 > 0):
                    pool.wait_ge(norm_ready, g4)
                nc.gpsimd.tensor_scalar(minus_mean[:, rows], y_sum[:, rows], -1.0 / D, None, ALU.mult)\
                    .then_inc(mean_done, 2)

            def norm(g4, half):
                rows = slice(2 * half, 2 * half + 2)
                n = done(g4, 2 * half + 2)
                pool.wait_ge(dev_done, n)
                nc.gpsimd.tensor_scalar(var_eps[:, rows], dev_sum[:, rows], 1.0 / D, LN_EPS, ALU.mult, ALU.add)\
                    .then_inc(eps_done, 2)
                if half == 0 and (not isinstance(g4, int) or g4 > 0):
                    pool.wait_ge(res_ready, g4)
                pool.wait_ge(eps_done, n)
                nc.gpsimd.tensor_tensor(rstd[:, rows], var_eps[:, rows], minus_half[:, :], ALU.pow)\
                    .then_inc(rstd_done, 2)
                pool.wait_ge(mean_done, n)
                pool.wait_ge(rstd_done, n)
                nc.gpsimd.tensor_tensor(shift[:, rows], minus_mean[:, rows], rstd[:, rows], ALU.mult)\
                    .then_inc(norm_ready, 2)

            def both(g4):
                mean(g4, 0)
                mean(g4, 1)
                norm(g4, 0)
                norm(g4, 1)

            both(0)
            with pool.Fori(4, 4 * G - 4, 4) as g4:
                both(g4)
            norm(4 * G - 4, 0)
            norm(4 * G - 4, 1)

        @block.tensor
        def _(pe):
            def products_a(g4, u, blocks):
                for b in blocks:
                    if b >= 2 or not isinstance(g4, int) or g4 >= 4:
                        pe.wait_ge(g2_ready, done(g4, b - 1))
                    rows = slice(b * P, (b + 1) * P)
                    for k in range(KB):
                        bank = ps_a[:, b % 2, :]
                        nc.tensor.matmul(bank, xT_hi[u][:, k, rows], w_hi[:, k, 0:WA], start=k == 0, stop=False)
                        nc.tensor.matmul(bank, xT_hi[u][:, k, rows], w_lo[:, k, 0:WA], start=False, stop=False)
                        end = nc.tensor.matmul(bank, xT_lo[u][:, k, rows], w_hi[:, k, 0:WA], start=False,
                                               stop=k == KB - 1)
                    end.then_inc(wa_done, 1)

            def products_b(g4, u, b, start=False):
                if isinstance(g4, int) and g4 == 0 and b % 2 == 0:
                    pe.wait_ge(x_split, done(g4, b + 2))
                elif b == 0:
                    pe.wait_ge(x_split, done(g4, 4))
                if not start:
                    pe.wait_ge(g0s_ready, done(g4, b))
                elif g4 > 0:
                    pe.wait_ge(g0s_ready, done(g4, b - 3))
                rows = slice(b * P, (b + 1) * P)
                bank = ps_u[:, b, 0:WB] if start else ps_b[:, 0:WB]
                for k in range(KB):
                    cols = slice(WA, WA + WB)
                    nc.tensor.matmul(bank, xT_hi[u][:, k, rows], w_hi[:, k, cols], start=k == 0, stop=False)
                    nc.tensor.matmul(bank, xT_hi[u][:, k, rows], w_lo[:, k, cols], start=False, stop=False)
                    end = nc.tensor.matmul(bank, xT_lo[u][:, k, rows], w_hi[:, k, cols], start=False,
                                           stop=k == KB - 1)
                end.then_inc(wb_done, 1)

            def spread_si(g4, u):
                pe.wait_ge(g0s_ready, done(g4, 4))
                if not isinstance(g4, int) or g4 > 0:
                    pe.wait_ge(exp_done, g4)
                for b in range(NB):
                    end = nc.tensor.transpose(ps_z[:, b * P:(b + 1) * P],
                                              g0s[u][:, b, SI:SI + 1].to_broadcast([P, P]), ident[:, :])
                end.then_inc(z_done, 4)

            def apply_1(g4, u, b, after_first=False, sources=range(NB)):
                if b == 0 and sources[0] == 0:
                    pe.wait_ge(f_ready, done(g4, 4))
                if sources[0] == 0:
                    if after_first:
                        pe.wait_ge(v_done, done(g4, b - 3))
                    elif not isinstance(g4, int) or g4 > 0:
                        pe.wait_ge(h_done, done(g4, b - 3))
                    else:
                        pe.wait_ge(g0s_ready, done(4, b + 1))
                cols = slice(b * P, (b + 1) * P)
                for j in sources:
                    if b == 0 and j % 2 == 0:
                        pe.wait_ge(al_ready, done(g4, j + 2))
                        pe.wait_ge(g2_ready, done(g4, j + 2))
                    nc.tensor.matmul(ps_u[:, b, 0:U1], al_hi[u][:, j, cols], g2_hi[u][:, j, :], start=j == 0,
                                     stop=False)
                    nc.tensor.matmul(ps_u[:, b, 0:U1], al_hi[u][:, j, cols], g2_lo[u][:, j, :], start=False,
                                     stop=False)
                    end = nc.tensor.matmul(ps_u[:, b, 0:U1], al_lo[u][:, j, cols], g2_hi[u][:, j, :], start=False,
                                           stop=j == NB - 1)
                if NB - 1 in sources:
                    end.then_inc(t1_done, 1)

            def apply_2(g4, u, b, sources=range(NB), bank=None):
                pe.wait_ge(v_ready, done(g4, max(sources) + 1))
                bank = ps_u[:, b, 0:D] if bank is None else bank
                cols = slice(b * P, (b + 1) * P)
                for j in sources:
                    nc.tensor.matmul(bank, al_hi[u][:, j, cols], v_hi[u][:, j, :], start=j == 0, stop=False)
                    nc.tensor.matmul(bank, al_hi[u][:, j, cols], v_lo[u][:, j, :], start=False, stop=False)
                    end = nc.tensor.matmul(bank, al_lo[u][:, j, cols], v_hi[u][:, j, :], start=False,
                                           stop=j == NB - 1)
                if NB - 1 in sources:
                    end.then_inc(t2_done, 1)

            ALL = range(NB)

            def warm_up(products):
                for _ in range(products):
                    nc.tensor.matmul(ps_a[:, 0, 0:P], ident[:, :], ident[:, :], start=True, stop=True)

            pe.wait_ge(ident_ready, 1)
            warm_up(WARM_UP[0])
            pe.wait_ge(v_loaded, 32)
            for k in range(KB):
                for e in range(KB):
                    end = nc.tensor.matmul(ps_z[:, 2 * k:2 * k + 2], wvT[:, e, k * P:(k + 1) * P], a_bv_sb[:, e, 0:2],
                                           start=e == 0, stop=e == KB - 1)
            end.then_inc(score_done, 1)
            warm_up(WARM_UP[1])
            pe.wait_ge(w_ready, 1)
            products_b(0, 0, 0, start=True)
            products_b(0, 0, 1, start=True)
            pe.wait_ge(rows_loaded, 32)
            nc.tensor.matmul(ps_b[:, 0:D + 2], ones[0:STEPS, :], bk_ab[:, :], start=True, stop=False)
            for e in range(KB):
                end = nc.tensor.matmul(ps_b[:, D:D + 2], a_bv_sb[:, e, 2:3].to_broadcast([P, P]), a_bv_sb[:, e, 0:2],
                                       start=False, stop=e == KB - 1)
            end.then_inc(bias_done, 1)
            products_b(0, 0, 2, start=True)
            products_b(0, 0, 3, start=True)
            pe.wait_ge(w_ready, 2)
            products_a(0, 0, [0])
            spread_si(0, 0)
            products_a(0, 0, ALL[1:3])
            products_b(4, 1, 0, start=True)
            products_b(4, 1, 1, start=True)
            products_a(0, 0, ALL[3:])
            products_b(4, 1, 2, start=True)
            products_b(4, 1, 3, start=True)
            for b in ALL:
                apply_1(0, 0, b, sources=ALL[:2])
            spread_si(4, 1)
            products_a(4, 1, [0])
            for b in ALL:
                apply_1(0, 0, b, sources=ALL[2:])
            with pe.Fori(0, LOOPED, 8) as pair4:
                for u in range(PAR):
                    g4 = pair4 + 4 * u
                    products_a(g4 + 4, 1 - u, ALL[1:3])
                    products_b(g4 + 8, u, 0)
                    products_a(g4 + 4, 1 - u, ALL[3:])
                    apply_2(g4, u, 0)
                    apply_2(g4, u, 1)
                    apply_2(g4, u, 2)
                    products_b(g4 + 8, u, 1)
                    apply_2(g4, u, 3)
                    products_b(g4 + 8, u, 2)
                    apply_1(g4 + 4, 1 - u, 0)
                    products_b(g4 + 8, u, 3)
                    apply_1(g4 + 4, 1 - u, 1)
                    spread_si(g4 + 8, u)
                    apply_1(g4 + 4, 1 - u, 2)
                    products_a(g4 + 8, u, [0])
                    apply_1(g4 + 4, 1 - u, 3)
            products_a(LOOPED + 4, 1, ALL[1:])
            for b in ALL[:3]:
                apply_2(LOOPED, 0, b)
            for b in ALL:
                apply_1(LOOPED + 4, 1, b, after_first=b == 3)
            pe.wait_ge(g0s_ready, 4 * G)
            apply_2(LOOPED, 0, 3, bank=ps_b[:, 0:D])
            for sources in (ALL[:2], ALL[2:]):
                for b in ALL:
                    if sources[0] == 0:
                        pe.wait_ge(v_done, done(LOOPED + 4, b + 1))
                    apply_2(LOOPED + 4, 1, b, sources)

        @block.scalar
        def _(act):
            def split_x(g4, u, loads):
                act.wait_ge(xT_loaded[u], loads)
                if not isinstance(g4, int) or g4 >= 8:
                    act.wait_ge(wa_done, done(g4, -4))
                nc.scalar.activation(xT_hi[u][:, :, :], xT_in[u][:, :, :], ACT.Copy).then_inc(xh_ready, 4)

            def leave_a(g4, u, b):
                act.wait_ge(wa_done, done(g4, b + 1))
                if b == 0 and (not isinstance(g4, int) or g4 >= 8):
                    act.wait_ge(t1_done, done(g4, -4))
                    act.wait_ge(v_done, done(g4, -4))
                f = factors[u][:, b, 0:1]
                nc.scalar.activation(g2_hi[u][:, b, 0:D], ps_a[:, b % 2, D:WA], ACT.Copy, scale=f)
                nc.scalar.activation(g1[u][:, b, :], ps_a[:, b % 2, 0:D], ACT.Copy, scale=f).then_inc(g1_ready, 1)

            def factor(g4, u):
                act.wait_ge(g0s_ready, done(g4, 4))
                if not isinstance(g4, int) or g4 >= 8:
                    act.wait_ge(v_done, done(g4, -4))
                nc.scalar.activation(factors[u][:, :, :], g0s[u][:, :, D:WB], ACT.Exp, scale=0.25)\
                    .then_inc(factors_done, 4)
                act.wait_ge(factors_done, done(g4, 4))
                nc.scalar.activation(g2_hi[u][:, :, D:U1], factors[u][:, :, :], ACT.Copy).then_inc(fh_ready, 4)

            def exponential(g4, u, b):
                if b == 0:
                    act.wait_ge(z_done, done(g4, 4))
                    if not isinstance(g4, int) or g4 > 0:
                        act.wait_ge(al_ready, g4)
                nc.scalar.activation(alpha[:, b, :], ps_z[:, :], ACT.Exp, scale=-1.0, bias=g0s[u][:, b, SJ:SJ + 1])\
                    .then_inc(exp_done, 1)

            def alpha_high(g4, u, half):
                act.wait_ge(alpha_done, done(g4, 2 * half + 2))
                if half == 0 and (not isinstance(g4, int) or g4 >= 8):
                    act.wait_ge(t2_done, done(g4, -4))
                rows = slice(2 * half, 2 * half + 2)
                nc.scalar.activation(al_hi[u][:, rows, :], alpha[:, rows, :], ACT.Copy).then_inc(alh_ready, 2)

            def v_high(g4, u, half):
                act.wait_ge(v_done, done(g4, 2 * half + 2))
                if half == 0 and (not isinstance(g4, int) or g4 >= 8):
                    act.wait_ge(t2_done, done(g4, -4))
                rows = slice(2 * half, 2 * half + 2)
                nc.scalar.activation(v_hi[u][:, rows, :], v[u][:, rows, :], ACT.Copy).then_inc(vh_ready, 2)

            def deviation(g4, u, b, stores=0):
                act.wait_ge(mean_done, done(g4, b + 1))
                if b == 0 and (not isinstance(g4, int) or g4 >= 8):
                    act.wait_ge(stored[u], stores)
                nc.scalar.activation(res[u][:, b, :], y[u][:, b, :], ACT.Square, bias=minus_mean[:, b:b + 1],
                                     accum_out=dev_sum[:, b:b + 1]).then_inc(dev_done, 1)

            def deviations(g4, u, half, stores=0):
                deviation(g4, u, 2 * half, stores)
                deviation(g4, u, 2 * half + 1)

            def normalise(g4, u, half, blocks=2):
                act.wait_ge(norm_ready, done(g4, 2 * half + 2))
                for b in range(2 * half, 2 * half + blocks):
                    nc.scalar.activation(res[u][:, b, :], y[u][:, b, :], ACT.Identity, bias=shift[:, b:b + 1],
                                         scale=rstd[:, b:b + 1]).then_inc(res_ready, 1)

            def store(q, g4, u):
                act.wait_ge(res_ready, done(g4, 4))
                act.dma_start(out_of[q, u], res[u][:, :, :].rearrange("p b d -> p (b d)")).then_inc(stored[u], 16)

            act.dma_start(a_bv_sb[:, :, :], a_bv).then_inc(v_loaded, 16)
            act.dma_start(xT_in[0][:, :, 0:HALF], xT_of[0, 0][:, :, 0:HALF]).then_inc(x0_loaded, 16)
            act.dma_start(xT_in[0][:, :, HALF:N], xT_of[0, 0][:, :, HALF:N]).then_inc(xT_loaded[0], 16)
            act.wait_ge(ident_ready, 1)
            nc.scalar.activation(warm[:, :], ident[:, 0:1], ACT.Exp)
            act.wait_ge(x0_loaded, 16)
            nc.scalar.activation(xT_hi[0][:, :, 0:HALF], xT_in[0][:, :, 0:HALF], ACT.Copy).then_inc(xh_ready, 2)
            act.wait_ge(setup, 2)
            act.wait_ge(w_loaded, 16)
            nc.scalar.activation(w_hi[:, :, WA:], w_raw[:, :, WA:], ACT.Copy).then_inc(w_hi_ready, 1)
            act.wait_ge(xT_loaded[0], 16)
            nc.scalar.activation(xT_hi[0][:, :, HALF:N], xT_in[0][:, :, HALF:N], ACT.Copy).then_inc(xh_ready, 2)
            act.wait_ge(w12_loaded, 32)
            nc.scalar.activation(w_hi[:, :, 0:WA], w_raw[:, :, 0:WA], ACT.Copy).then_inc(w_hi_ready, 1)
            split_x(4, 1, 16)
            factor(0, 0)
            leave_a(0, 0, 0)
            exponential(0, 0, 0)
            exponential(0, 0, 1)
            leave_a(0, 0, 1)
            exponential(0, 0, 2)
            alpha_high(0, 0, 0)
            exponential(0, 0, 3)
            leave_a(0, 0, 2)
            leave_a(0, 0, 3)
            alpha_high(0, 0, 1)
            factor(4, 1)
            split_x(8, 0, 32)
            for b in range(NB):
                exponential(4, 1, b)

            def finish(q, g4, u):
                normalise(g4, u, 0)
                normalise(g4, u, 1)
                store(q, g4, u)

            def step(q, g4, u, first=False, prepare=True, split=True, xT_loads=0, stores=0):
                leave_a(g4 + 4, 1 - u, 0)
                v_high(g4, u, 0)
                leave_a(g4 + 4, 1 - u, 1)
                v_high(g4, u, 1)
                leave_a(g4 + 4, 1 - u, 2)
                leave_a(g4 + 4, 1 - u, 3)
                alpha_high(g4 + 4, 1 - u, 0)
                alpha_high(g4 + 4, 1 - u, 1)
                if not first:
                    deviations(g4 - 4, 1 - u, 1)
                    finish(q, g4 - 4, 1 - u)
                if prepare:
                    factor(g4 + 8, u)
                if split:
                    split_x(g4 + 12, 1 - u, xT_loads)
                if prepare:
                    for b in range(NB):
                        exponential(g4 + 8, u, b)
                deviations(g4, u, 0, stores)

            LAST = G // PAR - 1
            step(0, 0, 0, first=True, xT_loads=32)
            step(0, 4, 1, xT_loads=48)
            with act.Fori(1, LAST - 1, 1) as q:
                step(q - 1, 8 * q, 0, xT_loads=16 * q + 32, stores=16 * q)
                step(q, 8 * q + 4, 1, xT_loads=16 * q + 48, stores=16 * q)
            step(LAST - 2, LOOPED - 8, 0, xT_loads=16 * LAST + 16, stores=16 * (LAST - 1))
            step(LAST - 1, LOOPED - 4, 1, split=False, stores=16 * (LAST - 1))

            leave_a(LOOPED + 4, 1, 0)
            v_high(LOOPED, 0, 0)
            leave_a(LOOPED + 4, 1, 1)
            v_high(LOOPED, 0, 1)
            leave_a(LOOPED + 4, 1, 2)
            alpha_high(LOOPED + 4, 1, 0)
            leave_a(LOOPED + 4, 1, 3)
            alpha_high(LOOPED + 4, 1, 1)
            deviations(LOOPED - 4, 1, 1)
            finish(LAST - 1, LOOPED - 4, 1)
            v_high(LOOPED + 4, 1, 0)
            deviations(LOOPED, 0, 0, 16 * LAST)
            v_high(LOOPED + 4, 1, 1)
            deviations(LOOPED, 0, 1)
            normalise(LOOPED, 0, 0)
            normalise(LOOPED, 0, 1)
            for b in range(NB):
                deviation(LOOPED + 4, 1, b, 16 * LAST)
            normalise(LOOPED + 4, 1, 0)
            normalise(LOOPED + 4, 1, 1, blocks=1)

        @block.vector
        def _(dve):
            def split_x(g4, u):
                dve.wait_ge(x_split, g4)
                dve.wait_ge(xh_ready, done(g4, 4))
                nc.vector.tensor_tensor(xT_lo[u][:, :, :], xT_in[u][:, :, :], xT_hi[u][:, :, :].bitcast(F32),
                                        ALU.subtract).then_inc(x_split, 4)

            def leave_b(g4, u, b, start=False):
                dve.wait_ge(wb_done, done(g4, b + 1))
                if not isinstance(g4, int) or g4 >= 8:
                    dve.wait_ge(h_done, done(g4, b - 7))
                bank = ps_u[:, b, 0:WB] if start else ps_b[:, 0:WB]
                nc.vector.tensor_tensor(g0s[u][:, b, :], bank, bias_row[:, :], ALU.add)\
                    .then_inc(g0s_ready, 1)

            def g2_low(g4, u, b):
                dve.wait_ge(g1_ready, done(g4, b + 1))
                nc.vector.scalar_tensor_tensor(g2_lo[u][:, b, 0:D], ps_a[:, b % 2, D:WA], factors[u][:, b, 0:1],
                                               g2_hi[u][:, b, 0:D].bitcast(F32), ALU.mult, ALU.subtract)\
                    .then_inc(g2_ready, 1)

            def f_low(g4, u):
                dve.wait_ge(fh_ready, done(g4, 4))
                nc.vector.tensor_tensor(g2_lo[u][:, :, D:U1], factors[u][:, :, :],
                                        g2_hi[u][:, :, D:U1].bitcast(F32), ALU.subtract).then_inc(f_ready, 4)

            def times_adj(g4, u, half, loads=0):
                dve.wait_ge(exp_done, done(g4, 2 * half + 2))
                if half == 0:
                    dve.wait_ge(adj_loaded[u], loads)
                two = alpha[:, 2 * half:2 * half + 2, :]
                nc.vector.scalar_tensor_tensor(two, two, 1.0, adj_in[u][:, 2 * half:2 * half + 2, :], ALU.max,
                                               ALU.mult)\
                    .then_inc(alpha_done, 2)

            def alpha_low(g4, u, half):
                dve.wait_ge(alh_ready, done(g4, 2 * half + 2))
                rows = slice(2 * half, 2 * half + 2)
                nc.vector.tensor_tensor(al_lo[u][:, rows, :], alpha[:, rows, :], al_hi[u][:, rows, :].bitcast(F32),
                                        ALU.subtract).then_inc(al_ready, 2)

            def row_sums(g4, u, half):
                rows = slice(2 * half, 2 * half + 2)
                dve.wait_ge(t1_done, done(g4, 2 * half + 2))
                nc.vector.scalar_tensor_tensor(denom[:, rows], factors[u][:, rows, 1], ROWSUM_EPS, ps_u[:, rows, D],
                                               ALU.mult, ALU.add).then_inc(denom_done, 2)

            def invert(g4, u, half):
                rows = slice(2 * half, 2 * half + 2)
                dve.wait_ge(denom_done, done(g4, 2 * half + 2))
                nc.vector.reciprocal(rcp[u][:, rows], denom[:, rows]).then_inc(rcp_done, 2)

            def invert_f(g4, u, half):
                rows = slice(2 * half, 2 * half + 2)
                dve.wait_ge(rcp_done, done(g4, 2 * half + 2))
                nc.vector.tensor_tensor(rcp_f[:, rows], rcp[u][:, rows], factors[u][:, rows, 0], ALU.mult)\
                    .then_inc(rcpf_done, 2)

            def combine(g4, u, half):
                dve.wait_ge(rcpf_done, done(g4, 2 * half + 2))
                for b in range(2 * half, 2 * half + 2):
                    nc.vector.scalar_tensor_tensor(v[u][:, b, :], ps_u[:, b, 0:D], rcp_f[:, b:b + 1], g1[u][:, b, :],
                                                   ALU.mult, ALU.add).then_inc(v_done, 1)

            def v_low(g4, u, half):
                dve.wait_ge(vh_ready, done(g4, 2 * half + 2))
                rows = slice(2 * half, 2 * half + 2)
                nc.vector.tensor_tensor(v_lo[u][:, rows, :], v[u][:, rows, :], v_hi[u][:, rows, :].bitcast(F32),
                                        ALU.subtract).then_inc(v_ready, 2)

            def hidden(g4, u, b, bank=None):
                dve.wait_ge(t2_done, done(g4, b + 1))
                bank = ps_u[:, b, 0:D] if bank is None else bank
                nc.vector.scalar_tensor_tensor(h[:, b, :], bank, rcp[u][:, b:b + 1], g0s[u][:, b, 0:D],
                                               ALU.mult, ALU.add).then_inc(h_done, 1)

            def residual(g4, u, b, loads):
                dve.wait_ge(h_done, done(g4, b + 1))
                if b == 0:
                    dve.wait_ge(x_loaded[u], loads)
                    if not isinstance(g4, int) or g4 > 0:
                        dve.wait_ge(mean_done, g4)
                    if not isinstance(g4, int) or g4 >= 8:
                        dve.wait_ge(res_ready, done(g4, -4))
                nc.vector.scalar_tensor_tensor(y[u][:, b, :], h[:, b, :], 0.0, x_in[u][:, b, :], ALU.max, ALU.add,
                                               accum_out=y_sum[:, b:b + 1]).then_inc(y_done, 1)

            dve.wait_ge(score_done, 1)
            for a, scale in enumerate((0.8, -0.8)):
                nc.vector.tensor_scalar(w_raw[:, :, WA + D + a],
                                        ps_z[:, 0:2 * KB].rearrange("p (k a) -> p k a", a=2)[:, :, a], scale, None,
                                        ALU.mult).then_inc(setup, 1)

            def first_split(half):
                nodes = slice(half * HALF, (half + 1) * HALF)
                dve.wait_ge(xh_ready, 2 * half + 2)
                nc.vector.tensor_tensor(xT_lo[0][:, :, nodes], xT_in[0][:, :, nodes],
                                        xT_hi[0][:, :, nodes].bitcast(F32), ALU.subtract).then_inc(x_split, 2)

            first_split(0)
            dve.wait_ge(w_hi_ready, 1)
            nc.vector.tensor_tensor(w_lo[:, :, WA:], w_raw[:, :, WA:], w_hi[:, :, WA:].bitcast(F32), ALU.subtract)\
                .then_inc(w_ready, 1)
            first_split(1)
            dve.wait_ge(w_hi_ready, 2)
            nc.vector.tensor_tensor(w_lo[:, :, 0:WA], w_raw[:, :, 0:WA], w_hi[:, :, 0:WA].bitcast(F32), ALU.subtract)\
                .then_inc(w_ready, 1)
            dve.wait_ge(bias_done, 1)
            nc.vector.tensor_copy(bias_row[:, 0:WB], ps_b[:, 0:WB]).then_inc(setup, 1)
            dve.wait_ge(setup, 3)
            nc.vector.tensor_tensor(c_col[:, :], bias_row[:, SJ:SJ + 1], bias_row[:, SI:SI + 1], ALU.add)\
                .then_inc(setup, 1)
            dve.wait_ge(setup, 4)
            nc.vector.tensor_scalar(bias_row[:, SJ:SJ + 1], c_col[:, :], 0.8, None, ALU.mult).then_inc(setup, 1)
            nc.vector.memset(bias_row[:, SI:SI + 1], 0.0).then_inc(setup, 1)
            dve.wait_ge(setup, 6)
            leave_b(0, 0, 0, start=True)
            leave_b(0, 0, 1, start=True)
            leave_b(0, 0, 2, start=True)
            leave_b(0, 0, 3, start=True)
            f_low(0, 0)
            g2_low(0, 0, 0)
            times_adj(0, 0, 0, 16)
            g2_low(0, 0, 1)
            leave_b(4, 1, 0, start=True)
            alpha_low(0, 0, 0)
            leave_b(4, 1, 1, start=True)
            times_adj(0, 0, 1)
            g2_low(0, 0, 2)
            leave_b(4, 1, 2, start=True)
            g2_low(0, 0, 3)
            leave_b(4, 1, 3, start=True)
            alpha_low(0, 0, 1)
            times_adj(4, 1, 0, 16)
            row_sums(0, 0, 0)
            invert(0, 0, 0)
            invert_f(0, 0, 0)
            combine(0, 0, 0)

            def step(g4, u, prepare=True, split=True, x_loads=0, adj_loads=0):
                f_low(g4 + 4, 1 - u)
                g2_low(g4 + 4, 1 - u, 0)
                row_sums(g4, u, 1)
                invert(g4, u, 1)
                invert_f(g4, u, 1)
                combine(g4, u, 1)
                g2_low(g4 + 4, 1 - u, 1)
                v_low(g4, u, 0)
                v_low(g4, u, 1)
                g2_low(g4 + 4, 1 - u, 2)
                times_adj(g4 + 4, 1 - u, 1)
                g2_low(g4 + 4, 1 - u, 3)
                hidden(g4, u, 0)
                if prepare:
                    leave_b(g4 + 8, u, 0)
                alpha_low(g4 + 4, 1 - u, 0)
                hidden(g4, u, 1)
                if prepare:
                    leave_b(g4 + 8, u, 1)
                alpha_low(g4 + 4, 1 - u, 1)
                hidden(g4, u, 2)
                residual(g4, u, 0, x_loads)
                hidden(g4, u, 3)
                if prepare:
                    leave_b(g4 + 8, u, 2)
                residual(g4, u, 1, x_loads)
                residual(g4, u, 2, x_loads)
                if prepare:
                    leave_b(g4 + 8, u, 3)
                residual(g4, u, 3, x_loads)
                if split:
                    split_x(g4 + 12, 1 - u)
                if prepare:
                    times_adj(g4 + 8, u, 0, adj_loads)
                row_sums(g4 + 4, 1 - u, 0)
                invert(g4 + 4, 1 - u, 0)
                invert_f(g4 + 4, 1 - u, 0)
                combine(g4 + 4, 1 - u, 0)

            step(0, 0, x_loads=16, adj_loads=32)
            step(4, 1, x_loads=16, adj_loads=32)
            with dve.Fori(8, LOOPED - 8, 8) as pair4:
                for u in range(PAR):
                    step(pair4 + 4 * u, u, x_loads=2 * pair4 + 16, adj_loads=2 * pair4 + 32)
            step(LOOPED - 8, 0, x_loads=8 * G - 16, adj_loads=8 * G)
            step(LOOPED - 4, 1, split=False, x_loads=8 * G - 16, adj_loads=8 * G)

            f_low(LOOPED + 4, 1)
            g2_low(LOOPED + 4, 1, 0)
            row_sums(LOOPED, 0, 1)
            invert(LOOPED, 0, 1)
            invert_f(LOOPED, 0, 1)
            combine(LOOPED, 0, 1)
            g2_low(LOOPED + 4, 1, 1)
            v_low(LOOPED, 0, 0)
            v_low(LOOPED, 0, 1)
            g2_low(LOOPED + 4, 1, 2)
            times_adj(LOOPED + 4, 1, 1)
            alpha_low(LOOPED + 4, 1, 0)
            g2_low(LOOPED + 4, 1, 3)
            hidden(LOOPED, 0, 0)
            alpha_low(LOOPED + 4, 1, 1)
            hidden(LOOPED, 0, 1)
            residual(LOOPED, 0, 0, 8 * G)
            residual(LOOPED, 0, 1, 8 * G)
            hidden(LOOPED, 0, 2)
            residual(LOOPED, 0, 2, 8 * G)
            row_sums(LOOPED + 4, 1, 0)
            invert(LOOPED + 4, 1, 0)
            invert_f(LOOPED + 4, 1, 0)
            combine(LOOPED + 4, 1, 0)
            v_low(LOOPED + 4, 1, 0)
            row_sums(LOOPED + 4, 1, 1)
            invert(LOOPED + 4, 1, 1)
            invert_f(LOOPED + 4, 1, 1)
            combine(LOOPED + 4, 1, 1)
            hidden(LOOPED, 0, 3, bank=ps_b[:, 0:D])
            residual(LOOPED, 0, 3, 8 * G)
            v_low(LOOPED + 4, 1, 1)

            def last_mean(b):
                dve.wait_ge(y_done, done(LOOPED + 4, b + 1))
                if b == 0:
                    dve.wait_ge(norm_ready, LOOPED + 4)
                nc.vector.tensor_scalar(minus_mean[:, b:b + 1], y_sum[:, b:b + 1], -1.0 / D, None, ALU.mult)\
                    .then_inc(mean_done, 1)

            hidden(LOOPED + 4, 1, 0)
            hidden(LOOPED + 4, 1, 1)
            residual(LOOPED + 4, 1, 0, 8 * G)
            hidden(LOOPED + 4, 1, 2)
            residual(LOOPED + 4, 1, 1, 8 * G)
            last_mean(0)
            hidden(LOOPED + 4, 1, 3)
            last_mean(1)
            residual(LOOPED + 4, 1, 2, 8 * G)
            last_mean(2)
            residual(LOOPED + 4, 1, 3, 8 * G)
            last_mean(3)
            dve.wait_ge(norm_ready, 4 * G)
            nc.vector.tensor_scalar(res[1][:, 3, :], y[1][:, 3, :], rstd[:, 3:4], shift[:, 3:4], ALU.mult, ALU.add)\
                .then_inc(last_block, 1)


def kernel(x, adj, L0_gnn_Wv, L0_gnn_bv, L0_gnn_aw, L0_gnn_ab, L0_gnn_Wk, L0_gnn_bk):
    import numpy as np
    import concourse.bacc as bacc
    from concourse.bass_utils import run_bass_kernel_spmd

    x, adj = np.asarray(x), np.asarray(adj)
    G, N, D = x.shape
    NB, KB = N // P, D // P
    xT = np.ascontiguousarray(x.reshape(G, P, NB, KB, P).transpose(0, 4, 3, 2, 1)).reshape(G, P, KB, N)
    adjT = np.ascontiguousarray(adj.reshape(G, P, NB, P, NB).transpose(0, 3, 4, 2, 1)).reshape(G, P, NB, N)
    WvT = np.asarray(L0_gnn_Wv).T.reshape(KB, P, D).transpose(1, 0, 2)
    aw, bv = np.asarray(L0_gnn_aw).reshape(2, KB, P), np.asarray(L0_gnn_bv).reshape(1, KB, P)
    a_bv = np.concatenate([aw, bv]).transpose(2, 1, 0)
    arrays = {"xT": xT, "adjT": adjT, "x": x, "WvT": WvT, "a_bv": a_bv, "ab": L0_gnn_ab, "Wk": L0_gnn_Wk,
              "bk": L0_gnn_bk}
    arrays = {k: np.ascontiguousarray(a) for k, a in arrays.items()}
    nc = bacc.Bacc("TRN2", target_bir_lowering=False, num_devices=1)
    ins = [nc.dram_tensor(f"{k}_dram", a.shape, mybir.dt.from_np(a.dtype), kind="ExternalInput").ap()
           for k, a in arrays.items()]
    out = nc.dram_tensor("out_dram", x.shape, F32, kind="ExternalOutput").ap()
    build(nc, *ins, out)
    r = run_bass_kernel_spmd(nc, [{f"{k}_dram": a for k, a in arrays.items()}], core_ids=[0])
    return r.results[0]["out_dram"]
```
